# Optimizing a Trainium2 kernel written in Bass

```python
import numpy as np
import jax
import jax.numpy as jnp

def _softmax(x, axis=-1):
    return jax.nn.softmax(x, axis=axis)

def _gelu(x):
    return jax.nn.gelu(x, approximate=True)

def _silu(x):
    return jax.nn.silu(x)

def _sigmoid(x):
    return jax.nn.sigmoid(x)

def _layernorm(x, axis=-1, eps=1e-05):
    m = jnp.mean(x, axis=axis, keepdims=True)
    v = jnp.var(x, axis=axis, keepdims=True)
    return (x - m) / jnp.sqrt(v + eps)

def _scatter_add(tgt, idx, src, axis=0):
    return tgt.at[idx].add(src)

def _segment_sum(src, seg, n):
    return jax.ops.segment_sum(src, seg, n)
kernel_name = 'mk_seq_preln_d2_jaxref_r8_4ccac1'

def setup_inputs(seed: int=0):
    np.random.seed(seed)
    _w = jnp.asarray

    def _L0_attn_setup():
        import jax, jax.numpy as jnp
        import numpy as np
        B, L, C, H = (8, 256, 128, 16)
        HID = 4 * C

        def _rope(x):
            b, n, c = x.shape
            k_max = c // 2
            theta = 1.0 / 10000.0 ** (jnp.arange(k_max, dtype=jnp.float32) / k_max)
            cos_t, sin_t = (jnp.cos(theta), jnp.sin(theta))
            xr = x.reshape(b, n, k_max, 2)
            re = xr[..., 0] * cos_t - xr[..., 1] * sin_t
            im = xr[..., 0] * sin_t + xr[..., 1] * cos_t
            return jnp.stack((re, im), axis=-1).reshape(b, n, c)

        def _dwconv(x_bcl, w, bias):
            y = jax.lax.conv_general_dilated(x_bcl, w, (1,), [(1, 1)], dimension_numbers=('NCH', 'OIH', 'NCH'), feature_group_count=x_bcl.shape[1])
            return y + bias[None, :, None]

        def _ln(x, g, b, eps=1e-05):
            mu = x.mean(-1, keepdims=True)
            var = ((x - mu) ** 2).mean(-1, keepdims=True)
            return (x - mu) * jax.lax.rsqrt(var + eps) * g + b

        def _mlla_forward(x, cpe1_w, cpe1_b, norm1_g, norm1_b, in_w, in_b, actp_w, actp_b, dwc_w, dwc_b, qk_w, qk_b, lepe_w, lepe_b, out_w, out_b, cpe2_w, cpe2_b, norm2_g, norm2_b, fc1_w, fc1_b, fc2_w, fc2_b):
            b, n, c = x.shape
            h, d = (H, c // H)
            x = x + _dwconv(x.transpose(0, 2, 1), cpe1_w, cpe1_b).transpose(0, 2, 1)
            shortcut = x
            xn = _ln(x, norm1_g, norm1_b)
            act_res = jax.nn.silu(xn @ actp_w + actp_b)
            xi = xn @ in_w + in_b
            xi = jax.nn.silu(_dwconv(xi.transpose(0, 2, 1), dwc_w, dwc_b)).transpose(0, 2, 1)
            qk = xi @ qk_w + qk_b
            q = jax.nn.elu(qk[..., :c]) + 1.0
            k = jax.nn.elu(qk[..., c:]) + 1.0
            q_rope = _rope(q).reshape(b, n, h, d).transpose(0, 2, 1, 3)
            k_rope = _rope(k).reshape(b, n, h, d).transpose(0, 2, 1, 3)
            qh = q.reshape(b, n, h, d).transpose(0, 2, 1, 3)
            kh = k.reshape(b, n, h, d).transpose(0, 2, 1, 3)
            vh = xi.reshape(b, n, h, d).transpose(0, 2, 1, 3)
            k_mean = kh.mean(axis=2, keepdims=True)
            z = 1.0 / (jnp.einsum('bhnd,bhmd->bhnm', qh, k_mean) + 1e-06)
            kv = jnp.einsum('bhnd,bhne->bhde', k_rope, vh) * (1.0 / n)
            attn = jnp.einsum('bhnd,bhde->bhne', q_rope, kv) * z
            attn = attn.transpose(0, 2, 1, 3).reshape(b, n, c)
            v_bcl = vh.transpose(0, 2, 1, 3).reshape(b, n, c).transpose(0, 2, 1)
            attn = attn + _dwconv(v_bcl, lepe_w, lepe_b).transpose(0, 2, 1)
            x = shortcut + attn * act_res @ out_w + out_b
            x = x + _dwconv(x.transpose(0, 2, 1), cpe2_w, cpe2_b).transpose(0, 2, 1)
            xn2 = _ln(x, norm2_g, norm2_b)
            mlp = jax.nn.gelu(xn2 @ fc1_w + fc1_b, approximate=False) @ fc2_w + fc2_b
            return x + mlp
        key = jax.random.key(seed)
        ks = jax.random.split(key, 12)

        def nrm(k, shape, scale=0.02):
            return jax.random.normal(k, shape, jnp.float32) * scale
        return {'x': jax.random.normal(ks[0], (B, L, C), jnp.float32), 'cpe1_w': nrm(ks[1], (C, 1, 3), 0.1), 'cpe1_b': jnp.zeros((C,), jnp.float32), 'norm1_g': jnp.ones((C,), jnp.float32), 'norm1_b': jnp.zeros((C,), jnp.float32), 'in_w': nrm(ks[2], (C, C)), 'in_b': jnp.zeros((C,), jnp.float32), 'actp_w': nrm(ks[3], (C, C)), 'actp_b': jnp.zeros((C,), jnp.float32), 'dwc_w': nrm(ks[4], (C, 1, 3), 0.1), 'dwc_b': jnp.zeros((C,), jnp.float32), 'qk_w': nrm(ks[5], (C, 2 * C)), 'qk_b': jnp.zeros((2 * C,), jnp.float32), 'lepe_w': nrm(ks[6], (C, 1, 3), 0.1), 'lepe_b': jnp.zeros((C,), jnp.float32), 'out_w': nrm(ks[7], (C, C)), 'out_b': jnp.zeros((C,), jnp.float32), 'cpe2_w': nrm(ks[8], (C, 1, 3), 0.1), 'cpe2_b': jnp.zeros((C,), jnp.float32), 'norm2_g': jnp.ones((C,), jnp.float32), 'norm2_b': jnp.zeros((C,), jnp.float32), 'fc1_w': nrm(ks[9], (C, HID)), 'fc1_b': jnp.zeros((HID,), jnp.float32), 'fc2_w': nrm(ks[10], (HID, C)), 'fc2_b': jnp.zeros((C,), jnp.float32)}
    _L0_attn_in = _L0_attn_setup()

    def _L0_ffn_setup():
        import jax, jax.numpy as jnp
        import numpy as np
        TOP_K = 8
        key = jax.random.key(seed)
        ks = jax.random.split(key, 6)
        B, S, D, F, E = (2, 128, 128, 64, 64)
        x = jax.random.normal(ks[0], (B, S, D), dtype=jnp.float32)
        centroids = jax.random.normal(ks[1], (E, D), dtype=jnp.float32) * 0.05
        expert_biases = jnp.zeros((E,), dtype=jnp.float32)
        Ws_up = jax.random.normal(ks[2], (D, F), dtype=jnp.float32) / np.sqrt(D)
        Ws_down = jax.random.normal(ks[3], (F, D), dtype=jnp.float32) / np.sqrt(F)
        W_up = jax.random.normal(ks[4], (E, D, F), dtype=jnp.float32) / np.sqrt(D)
        W_down = jax.random.normal(ks[5], (E, F, D), dtype=jnp.float32) / np.sqrt(F)
        return {'x': x, 'centroids': centroids, 'expert_biases': expert_biases, 'Ws_up': Ws_up, 'Ws_down': Ws_down, 'W_up': W_up, 'W_down': W_down}
    _L0_ffn_in = _L0_ffn_setup()

    def _L1_attn_setup():
        import jax, jax.numpy as jnp
        import numpy as np
        import math
        DIM = 128
        HEADS = 16
        B, N = (2, 256)
        POLY = jnp.array([-0.037, 0.481, -2.3, 4.917, -1.791], dtype=jnp.float32)

        def adaptive_temperature_softmax(logits):
            original_probs = jax.nn.softmax(logits, axis=-1)
            entropy = jnp.sum(-original_probs * jnp.log(original_probs + 1e-09), axis=-1, keepdims=True)
            e2 = entropy * entropy
            poly_result = POLY[0] * e2 * e2 + POLY[1] * e2 * entropy + POLY[2] * e2 + POLY[3] * entropy + POLY[4]
            beta = jnp.where(entropy > 0.5, jnp.maximum(poly_result, 1.0), 1.0)
            return jax.nn.softmax(logits * beta, axis=-1)
        key = jax.random.key(seed)
        ks = jax.random.split(key, 5)
        s = 1.0 / math.sqrt(DIM)
        return {'x': jax.random.normal(ks[0], (B, N, DIM), dtype=jnp.float32), 'Wq': jax.random.normal(ks[1], (DIM, DIM), dtype=jnp.float32) * s, 'Wk': jax.random.normal(ks[2], (DIM, DIM), dtype=jnp.float32) * s, 'Wv': jax.random.normal(ks[3], (DIM, DIM), dtype=jnp.float32) * s, 'Wo': jax.random.normal(ks[4], (DIM, DIM), dtype=jnp.float32) * s, 'bo': jnp.zeros((DIM,), dtype=jnp.float32)}
    _L1_attn_in = _L1_attn_setup()

    def _L1_ffn_setup():
        import jax, jax.numpy as jnp
        import numpy as np
        LN_EPS = 1e-05

        def layer_norm(x, g, b):
            mu = jnp.mean(x, axis=-1, keepdims=True)
            var = jnp.var(x, axis=-1, keepdims=True)
            return (x - mu) / jnp.sqrt(var + LN_EPS) * g + b

        def balanced_assignment(scores):
            T, E = scores.shape
            C = T // E
            taken = jnp.zeros((T,), dtype=bool)
            parts = []
            for e in range(E):
                s = jnp.where(taken, -jnp.inf, scores[:, e])
                _, idx = jax.lax.top_k(s, C)
                parts.append(idx)
                taken = taken.at[idx].set(True)
            return jnp.concatenate(parts)
        key = jax.random.key(seed)
        ks = jax.random.split(key, 4)
        B, S, D, F, E = (4, 256, 128, 512, 8)
        return {'x': jax.random.normal(ks[0], (B, S, D), dtype=jnp.float32), 'centroids': jax.random.normal(ks[1], (E, D), dtype=jnp.float32) * 0.1, 'ln_g': jnp.ones((D,), dtype=jnp.float32), 'ln_b': jnp.zeros((D,), dtype=jnp.float32), 'w1': jax.random.normal(ks[2], (E, D, F), dtype=jnp.float32) * 0.02, 'b1': jnp.zeros((E, F), dtype=jnp.float32), 'w2': jax.random.normal(ks[3], (E, F, D), dtype=jnp.float32) * 0.02, 'b2': jnp.zeros((E, D), dtype=jnp.float32)}
    _L1_ffn_in = _L1_ffn_setup()
    _d = {'L0_attn_x': _L0_attn_in['x'], 'L0_attn_cpe1_w': _L0_attn_in['cpe1_w'], 'L0_attn_cpe1_b': _L0_attn_in['cpe1_b'], 'L0_attn_norm1_g': _L0_attn_in['norm1_g'], 'L0_attn_norm1_b': _L0_attn_in['norm1_b'], 'L0_attn_in_w': _L0_attn_in['in_w'], 'L0_attn_in_b': _L0_attn_in['in_b'], 'L0_attn_actp_w': _L0_attn_in['actp_w'], 'L0_attn_actp_b': _L0_attn_in['actp_b'], 'L0_attn_dwc_w': _L0_attn_in['dwc_w'], 'L0_attn_dwc_b': _L0_attn_in['dwc_b'], 'L0_attn_qk_w': _L0_attn_in['qk_w'], 'L0_attn_qk_b': _L0_attn_in['qk_b'], 'L0_attn_lepe_w': _L0_attn_in['lepe_w'], 'L0_attn_lepe_b': _L0_attn_in['lepe_b'], 'L0_attn_out_w': _L0_attn_in['out_w'], 'L0_attn_out_b': _L0_attn_in['out_b'], 'L0_attn_cpe2_w': _L0_attn_in['cpe2_w'], 'L0_attn_cpe2_b': _L0_attn_in['cpe2_b'], 'L0_attn_norm2_g': _L0_attn_in['norm2_g'], 'L0_attn_norm2_b': _L0_attn_in['norm2_b'], 'L0_attn_fc1_w': _L0_attn_in['fc1_w'], 'L0_attn_fc1_b': _L0_attn_in['fc1_b'], 'L0_attn_fc2_w': _L0_attn_in['fc2_w'], 'L0_attn_fc2_b': _L0_attn_in['fc2_b'], 'L0_ffn_centroids': _L0_ffn_in['centroids'], 'L0_ffn_expert_biases': _L0_ffn_in['expert_biases'], 'L0_ffn_Ws_up': _L0_ffn_in['Ws_up'], 'L0_ffn_Ws_down': _L0_ffn_in['Ws_down'], 'L0_ffn_W_up': _L0_ffn_in['W_up'], 'L0_ffn_W_down': _L0_ffn_in['W_down'], 'L1_attn_Wq': _L1_attn_in['Wq'], 'L1_attn_Wk': _L1_attn_in['Wk'], 'L1_attn_Wv': _L1_attn_in['Wv'], 'L1_attn_Wo': _L1_attn_in['Wo'], 'L1_attn_bo': _L1_attn_in['bo'], 'L1_ffn_centroids': _L1_ffn_in['centroids'], 'L1_ffn_ln_g': _L1_ffn_in['ln_g'], 'L1_ffn_ln_b': _L1_ffn_in['ln_b'], 'L1_ffn_w1': _L1_ffn_in['w1'], 'L1_ffn_b1': _L1_ffn_in['b1'], 'L1_ffn_w2': _L1_ffn_in['w2'], 'L1_ffn_b2': _L1_ffn_in['b2']}
    _x0 = _d['L0_attn_x']
    _d['L0_attn_x'] = jax.random.normal(jax.random.fold_in(jax.random.key(seed), 1), (4, 1024, 128), dtype=_x0.dtype)
    del _x0
    return _d

def reference(L0_attn_x, L0_attn_cpe1_w, L0_attn_cpe1_b, L0_attn_norm1_g, L0_attn_norm1_b, L0_attn_in_w, L0_attn_in_b, L0_attn_actp_w, L0_attn_actp_b, L0_attn_dwc_w, L0_attn_dwc_b, L0_attn_qk_w, L0_attn_qk_b, L0_attn_lepe_w, L0_attn_lepe_b, L0_attn_out_w, L0_attn_out_b, L0_attn_cpe2_w, L0_attn_cpe2_b, L0_attn_norm2_g, L0_attn_norm2_b, L0_attn_fc1_w, L0_attn_fc1_b, L0_attn_fc2_w, L0_attn_fc2_b, L0_ffn_centroids, L0_ffn_expert_biases, L0_ffn_Ws_up, L0_ffn_Ws_down, L0_ffn_W_up, L0_ffn_W_down, L1_attn_Wq, L1_attn_Wk, L1_attn_Wv, L1_attn_Wo, L1_attn_bo, L1_ffn_centroids, L1_ffn_ln_g, L1_ffn_ln_b, L1_ffn_w1, L1_ffn_b1, L1_ffn_w2, L1_ffn_b2):

    def _L0_attn_ref(x, cpe1_w, cpe1_b, norm1_g, norm1_b, in_w, in_b, actp_w, actp_b, dwc_w, dwc_b, qk_w, qk_b, lepe_w, lepe_b, out_w, out_b, cpe2_w, cpe2_b, norm2_g, norm2_b, fc1_w, fc1_b, fc2_w, fc2_b):
        import jax, jax.numpy as jnp
        import numpy as np
        B, L, C, H = (8, 256, 128, 16)
        HID = 4 * C

        def _rope(x):
            b, n, c = x.shape
            k_max = c // 2
            theta = 1.0 / 10000.0 ** (jnp.arange(k_max, dtype=jnp.float32) / k_max)
            cos_t, sin_t = (jnp.cos(theta), jnp.sin(theta))
            xr = x.reshape(b, n, k_max, 2)
            re = xr[..., 0] * cos_t - xr[..., 1] * sin_t
            im = xr[..., 0] * sin_t + xr[..., 1] * cos_t
            return jnp.stack((re, im), axis=-1).reshape(b, n, c)

        def _dwconv(x_bcl, w, bias):
            y = jax.lax.conv_general_dilated(x_bcl, w, (1,), [(1, 1)], dimension_numbers=('NCH', 'OIH', 'NCH'), feature_group_count=x_bcl.shape[1])
            return y + bias[None, :, None]

        def _ln(x, g, b, eps=1e-05):
            mu = x.mean(-1, keepdims=True)
            var = ((x - mu) ** 2).mean(-1, keepdims=True)
            return (x - mu) * jax.lax.rsqrt(var + eps) * g + b

        def _mlla_forward(x, cpe1_w, cpe1_b, norm1_g, norm1_b, in_w, in_b, actp_w, actp_b, dwc_w, dwc_b, qk_w, qk_b, lepe_w, lepe_b, out_w, out_b, cpe2_w, cpe2_b, norm2_g, norm2_b, fc1_w, fc1_b, fc2_w, fc2_b):
            b, n, c = x.shape
            h, d = (H, c // H)
            x = x + _dwconv(x.transpose(0, 2, 1), cpe1_w, cpe1_b).transpose(0, 2, 1)
            shortcut = x
            xn = _ln(x, norm1_g, norm1_b)
            act_res = jax.nn.silu(xn @ actp_w + actp_b)
            xi = xn @ in_w + in_b
            xi = jax.nn.silu(_dwconv(xi.transpose(0, 2, 1), dwc_w, dwc_b)).transpose(0, 2, 1)
            qk = xi @ qk_w + qk_b
            q = jax.nn.elu(qk[..., :c]) + 1.0
            k = jax.nn.elu(qk[..., c:]) + 1.0
            q_rope = _rope(q).reshape(b, n, h, d).transpose(0, 2, 1, 3)
            k_rope = _rope(k).reshape(b, n, h, d).transpose(0, 2, 1, 3)
            qh = q.reshape(b, n, h, d).transpose(0, 2, 1, 3)
            kh = k.reshape(b, n, h, d).transpose(0, 2, 1, 3)
            vh = xi.reshape(b, n, h, d).transpose(0, 2, 1, 3)
            k_mean = kh.mean(axis=2, keepdims=True)
            z = 1.0 / (jnp.einsum('bhnd,bhmd->bhnm', qh, k_mean) + 1e-06)
            kv = jnp.einsum('bhnd,bhne->bhde', k_rope, vh) * (1.0 / n)
            attn = jnp.einsum('bhnd,bhde->bhne', q_rope, kv) * z
            attn = attn.transpose(0, 2, 1, 3).reshape(b, n, c)
            v_bcl = vh.transpose(0, 2, 1, 3).reshape(b, n, c).transpose(0, 2, 1)
            attn = attn + _dwconv(v_bcl, lepe_w, lepe_b).transpose(0, 2, 1)
            x = shortcut + attn * act_res @ out_w + out_b
            x = x + _dwconv(x.transpose(0, 2, 1), cpe2_w, cpe2_b).transpose(0, 2, 1)
            xn2 = _ln(x, norm2_g, norm2_b)
            mlp = jax.nn.gelu(xn2 @ fc1_w + fc1_b, approximate=False) @ fc2_w + fc2_b
            return x + mlp
        return _mlla_forward(x, cpe1_w, cpe1_b, norm1_g, norm1_b, in_w, in_b, actp_w, actp_b, dwc_w, dwc_b, qk_w, qk_b, lepe_w, lepe_b, out_w, out_b, cpe2_w, cpe2_b, norm2_g, norm2_b, fc1_w, fc1_b, fc2_w, fc2_b)

    def _L0_ffn_ref(x, centroids, expert_biases, Ws_up, Ws_down, W_up, W_down):
        import jax, jax.numpy as jnp
        import numpy as np
        TOP_K = 8
        B, S, D = x.shape
        E = centroids.shape[0]
        T = B * S
        xf = x.reshape(T, D)
        shared = jax.nn.silu(xf @ Ws_up) @ Ws_down
        aff = xf @ centroids.T
        biased = aff + expert_biases
        _, idx = jax.lax.top_k(biased, TOP_K)
        sel = jnp.take_along_axis(aff, idx, axis=1)
        w = jax.nn.sigmoid(sel)
        w = w / (jnp.sum(w, axis=-1, keepdims=True) + 1e-08)
        cw = jnp.zeros((T, E), dtype=x.dtype).at[jnp.arange(T)[:, None], idx].add(w)
        h = jax.nn.silu(jnp.einsum('td,edf->etf', xf, W_up))
        y = jnp.einsum('etf,efd->etd', h, W_down)
        routed = jnp.einsum('etd,te->td', y, cw)
        return (shared + routed).reshape(B, S, D)

    def _L1_attn_ref(x, Wq, Wk, Wv, Wo, bo):
        import jax, jax.numpy as jnp
        import numpy as np
        import math
        DIM = 128
        HEADS = 16
        B, N = (2, 256)
        POLY = jnp.array([-0.037, 0.481, -2.3, 4.917, -1.791], dtype=jnp.float32)

        def adaptive_temperature_softmax(logits):
            original_probs = jax.nn.softmax(logits, axis=-1)
            entropy = jnp.sum(-original_probs * jnp.log(original_probs + 1e-09), axis=-1, keepdims=True)
            e2 = entropy * entropy
            poly_result = POLY[0] * e2 * e2 + POLY[1] * e2 * entropy + POLY[2] * e2 + POLY[3] * entropy + POLY[4]
            beta = jnp.where(entropy > 0.5, jnp.maximum(poly_result, 1.0), 1.0)
            return jax.nn.softmax(logits * beta, axis=-1)
        b, n, d = x.shape
        h = HEADS
        hd = d // h

        def proj(W):
            t = x @ W.T
            return t.reshape(b, n, h, hd).transpose(0, 2, 1, 3)
        q, k, v = (proj(Wq), proj(Wk), proj(Wv))
        sim = jnp.einsum('bhid,bhjd->bhij', q, k) / math.sqrt(hd)
        neg = -jnp.finfo(sim.dtype).max
        causal = jnp.triu(jnp.ones((n, n), dtype=bool), k=1)
        sim = jnp.where(causal, neg, sim)
        attn = adaptive_temperature_softmax(sim)
        out = jnp.einsum('bhij,bhjd->bhid', attn, v)
        out = out.transpose(0, 2, 1, 3).reshape(b, n, d)
        return out @ Wo.T + bo

    def _L1_ffn_ref(x, centroids, ln_g, ln_b, w1, b1, w2, b2):
        import jax, jax.numpy as jnp
        import numpy as np
        LN_EPS = 1e-05

        def layer_norm(x, g, b):
            mu = jnp.mean(x, axis=-1, keepdims=True)
            var = jnp.var(x, axis=-1, keepdims=True)
            return (x - mu) / jnp.sqrt(var + LN_EPS) * g + b

        def balanced_assignment(scores):
            T, E = scores.shape
            C = T // E
            taken = jnp.zeros((T,), dtype=bool)
            parts = []
            for e in range(E):
                s = jnp.where(taken, -jnp.inf, scores[:, e])
                _, idx = jax.lax.top_k(s, C)
                parts.append(idx)
                taken = taken.at[idx].set(True)
            return jnp.concatenate(parts)
        D = x.shape[-1]
        feat = x.reshape(-1, D)
        T = feat.shape[0]
        E = centroids.shape[0]
        C = T // E
        norm = layer_norm(feat, ln_g, ln_b)
        scores = jax.lax.stop_gradient(norm @ centroids.T)
        sort_by_expert = balanced_assignment(scores)
        routed = feat[sort_by_expert].reshape(E, C, D)
        h = layer_norm(routed, ln_g, ln_b)
        h = jax.nn.gelu(jnp.einsum('ecd,edf->ecf', h, w1) + b1[:, None, :])
        h = jnp.einsum('ecf,efd->ecd', h, w2) + b2[:, None, :]
        out = routed + h
        inv = jnp.zeros((T,), dtype=jnp.int32).at[sort_by_expert].set(jnp.arange(T, dtype=jnp.int32))
        return out.reshape(T, D)[inv].reshape(x.shape)
    x = L0_attn_x
    x = x + _L0_attn_ref(_layernorm(x, axis=-1), L0_attn_cpe1_w, L0_attn_cpe1_b, L0_attn_norm1_g, L0_attn_norm1_b, L0_attn_in_w, L0_attn_in_b, L0_attn_actp_w, L0_attn_actp_b, L0_attn_dwc_w, L0_attn_dwc_b, L0_attn_qk_w, L0_attn_qk_b, L0_attn_lepe_w, L0_attn_lepe_b, L0_attn_out_w, L0_attn_out_b, L0_attn_cpe2_w, L0_attn_cpe2_b, L0_attn_norm2_g, L0_attn_norm2_b, L0_attn_fc1_w, L0_attn_fc1_b, L0_attn_fc2_w, L0_attn_fc2_b)
    x = x + _L0_ffn_ref(_layernorm(x, axis=-1), L0_ffn_centroids, L0_ffn_expert_biases, L0_ffn_Ws_up, L0_ffn_Ws_down, L0_ffn_W_up, L0_ffn_W_down)
    x = x + _L1_attn_ref(_layernorm(x, axis=-1), L1_attn_Wq, L1_attn_Wk, L1_attn_Wv, L1_attn_Wo, L1_attn_bo)
    x = x + _L1_ffn_ref(_layernorm(x, axis=-1), L1_ffn_centroids, L1_ffn_ln_g, L1_ffn_ln_b, L1_ffn_w1, L1_ffn_b1, L1_ffn_w2, L1_ffn_b2)
    return x

_drawn_inputs = setup_inputs


def setup_inputs(seed=0):
    import zlib

    import numpy as np

    out = dict(_drawn_inputs(seed))
    spreads = {'L0_attn_cpe1_b': (0.0, 0.1),
     'L0_attn_norm1_g': (1.0, 0.6),
     'L0_attn_norm1_b': (0.0, 0.8),
     'L0_attn_in_b': (0.0, 0.8),
     'L0_attn_actp_b': (0.0, 0.8),
     'L0_attn_dwc_b': (0.0, 0.8),
     'L0_attn_qk_b': (0.0, 2.0),
     'L0_attn_lepe_b': (0.0, 0.8),
     'L0_attn_out_b': (0.0, 0.8),
     'L0_attn_cpe2_b': (0.0, 0.8),
     'L0_attn_norm2_g': (1.0, 0.6),
     'L0_attn_norm2_b': (0.0, 2.0),
     'L0_attn_fc1_b': (0.0, 2.0),
     'L0_attn_fc2_b': (0.0, 0.8),
     'L0_ffn_expert_biases': (0.0, 0.8),
     'L1_attn_bo': (0.0, 0.8),
     'L1_ffn_ln_g': (1.0, 0.6),
     'L1_ffn_ln_b': (0.0, 2.0),
     'L1_ffn_b1': (0.0, 0.8),
     'L1_ffn_b2': (0.0, 0.8)}
    factors = {'L0_attn_in_w': 8.0,
     'L0_attn_actp_w': 8.0,
     'L0_attn_dwc_w': 8.0,
     'L0_attn_qk_w': 8.0,
     'L0_attn_lepe_w': 8.0,
     'L0_attn_out_w': 8.0,
     'L1_ffn_w1': 3.237,
     'L1_ffn_w2': 2.953,
     'L0_attn_fc1_w': 6.747,
     'L0_attn_fc2_w': 6.011,
     'L0_ffn_centroids': 4.624,
     'L0_ffn_W_up': 4.716,
     'L0_ffn_W_down': 4.38,
     'L1_attn_Wq': 3.949,
     'L1_attn_Wk': 3.682}
    for name, (base, spread) in spreads.items():
        noise = np.random.default_rng([zlib.crc32(name.encode()), seed]).standard_normal(out[name].shape)
        drawn = base * np.exp(spread * noise) if base else spread * noise
        out[name] = jnp.asarray(drawn.astype(out[name].dtype))
    for name, factor in factors.items():
        out[name] = (out[name] * factor).astype(out[name].dtype)
    return out
```

```python
import math
from contextlib import ExitStack

import concourse.bass as bass
import numpy as np
from concourse import mybir
from concourse.alu_op_type import AluOpType as ALU

ACT = mybir.ActivationFunctionType
AX = mybir.AxisListType
F32 = mybir.dt.float32
BF16 = mybir.dt.bfloat16

P = 128
BATCH, SEQ, CH = 4, 1024, 128
TILES = SEQ // P
EPS = 1e-5
HEADS, HEAD = 16, 8
BANK = 512
HALVES = SEQ // BANK
HID = 4 * CH
HIDS = HID // P
E0, F0 = 64, 64
PAIRS = E0 * F0 // P


class Signal:

    live = []

    def __init__(self, ctx, nc, name, per=1):
        self.sem = nc.alloc_semaphore(name)
        Signal.live.append(self.sem)
        self.per = per

    def at(self, turn, k=1):
        return turn * self.per + k


def retire(nc):
    with nc.Block() as block:
        @block.gpsimd
        def _(pool):
            for sem in Signal.live:
                pool.sem_clear(sem)
    for sem in Signal.live:
        nc.release_semaphore(sem)
    Signal.live.clear()


class Norm:

    def __init__(self, ctx, nc, name, buffers, per):
        self.summed = Signal(ctx, nc, name + "_summed", per)
        self.centered = Signal(ctx, nc, name + "_centered", per)
        self.squared = Signal(ctx, nc, name + "_squared", per)
        self.varied = Signal(ctx, nc, name + "_varied", per)
        self.logged = Signal(ctx, nc, name + "_logged", per)
        self.rooted = Signal(ctx, nc, name + "_rooted", per)
        self.scaled = Signal(ctx, nc, name + "_scaled", per)
        self.sums, self.cent, self.sq, self.var, self.log, self.rstd, self.eps = buffers

    def center(self, nc, dve, t, k, x):
        nc.vector.reduce_sum(self.sums[:, :], x, axis=AX.X).then_inc(self.summed.sem, 1)
        dve.wait_ge(self.summed.sem, self.summed.at(t, k))
        nc.vector.scalar_tensor_tensor(
            out=self.cent[:, :, :], in0=self.sums[:, :].unsqueeze(2).broadcast_to([P, TILES, CH]),
            scalar=-1.0 / CH, in1=x, op0=ALU.mult, op1=ALU.add).then_inc(self.centered.sem, 1)

    def square(self, nc, act, t, k):
        act.wait_ge(self.centered.sem, self.centered.at(t, k))
        nc.scalar.activation(self.sq[:, :, :], self.cent[:, :, :], ACT.Square).then_inc(self.squared.sem, 1)

    def variance(self, nc, dve, t, k):
        dve.wait_ge(self.squared.sem, self.squared.at(t, k))
        nc.vector.reduce_sum(self.var[:, :], self.sq[:, :, :], axis=AX.X).then_inc(self.varied.sem, 1)

    def root(self, nc, act, t, k, load=True):
        if load:
            nc.scalar.preload_act_table_set("natural_log_exp_and_others")
        act.wait_ge(self.varied.sem, self.varied.at(t, k))
        nc.scalar.activation(self.log[:, :], self.var[:, :], ACT.Ln, bias=self.eps[:, 0:1],
                             scale=1.0 / CH).then_inc(self.logged.sem, 1)
        act.wait_ge(self.logged.sem, self.logged.at(t, k))
        nc.scalar.activation(self.rstd[:, :], self.log[:, :], ACT.Exp, scale=-0.5).then_inc(self.rooted.sem, 1)

    def scale(self, nc, dve, t, k, out):
        dve.wait_ge(self.rooted.sem, self.rooted.at(t, k))
        nc.vector.tensor_tensor(out, self.cent[:, :, :], self.rstd[:, :].unsqueeze(2).broadcast_to([P, TILES, CH]),
                                ALU.mult).then_inc(self.scaled.sem, 1)


VECS, MATS1, MATS2, MATS3, MATS4 = {}, {}, {}, {}, {}
for table, items in (
    (VECS, [("cpe1_w", 3), ("cpe1_b", 1), ("norm1_g", 1), ("norm1_b", 1), ("in_b", 1), ("actp_b", 1),
            ("dwc_w", 3), ("dwc_b", 1), ("qk_b", 2), ("lepe_w", 3), ("lepe_b", 1), ("out_b", 1),
            ("cpe2_w", 3), ("cpe2_b", 1), ("norm2_g", 1), ("norm2_b", 1), ("fc1_b", HIDS), ("fc2_b", 1),
            ("ln_g", 1), ("ln_b", 1), ("b1", 32), ("b2", 8)]),
    (MATS1, [("ident", P), ("rope", P), ("rope_t", P), ("block", P), ("block16", HEADS),
             ("actp_w", CH), ("in_w", CH), ("qk_w", 2 * CH), ("out_w", CH), ("fc1_w", HID), ("fc2_w", HID)]),
    (MATS2, [("cent", E0), ("bias", E0), ("shared_up", F0), ("shared_down", CH),
             ("up", E0 * F0), ("down", E0 * F0)]),
    (MATS3, [("wq", CH), ("wk", CH), ("wv", CH), ("wo", CH), ("spread", CH), ("bo", CH)]),
    (MATS4, [("cent1", 8), ("ones", P), ("same", P), ("before", P), ("copies", 16), ("offsets", 8)]),
):
    at = 0
    for name, width in items:
        table[name] = (at, at + width)
        at += width
    table["all"] = (0, at)


def vec(tensor, name, k=0):
    a = VECS[name][0] + k
    return tensor[:, a:a + 1]


def mat(tensor, table, name, k=0, width=None, rows=P):
    a, b = table[name]
    if width is not None:
        a, b = a + k * width, a + (k + 1) * width
    return tensor[0:rows, a:b]


def linear_attention_block(nc, x, vecs, m1, eps):
    with ExitStack() as ctx:
        def sb(name, shape, dt=F32):
            return ctx.enter_context(nc.sbuf_tensor(name, shape, dt))

        def sig(name, per=1):
            return Signal(ctx, nc, name, per)

        ps = ctx.enter_context(nc.psum_tensor("la_ps", [P, 8, BANK], F32))

        def banks(k):
            flat = ps[:, 2 * k:2 * k + 2, :].rearrange("p a n -> p (a n)")
            return flat, flat.rearrange("p (t c) -> p t c", t=TILES)

        (psA, psA_tm), (psB, psB_tm), (psC, psC_tm), (psD, psD_tm) = (banks(k) for k in range(4))

        buffers = (sb("la_sums", [P, TILES]), sb("la_cent", [P, TILES, CH]), sb("la_sq", [P, TILES, CH]),
                   sb("la_var", [P, TILES]), sb("la_log", [P, TILES]), sb("la_rstd", [P, TILES]), eps)
        ln = Norm(ctx, nc, "la_ln", buffers, 3)
        y_tm = sb("la_y", [P, TILES, CH])
        u_pad = sb("la_u", [P, SEQ + 2])
        x2_pad = sb("la_x2", [P, SEQ + 2])
        xi_pad = sb("la_xi", [P, SEQ + 2])
        v_pad = sb("la_v", [P, SEQ + 2])
        x1 = sb("la_x1", [P, SEQ])
        x3 = sb("la_x3", [P, SEQ])
        xn = sb("la_xn", [P, SEQ])
        gate = sb("la_gate", [P, SEQ])
        conv = sb("la_conv", [P, SEQ])
        q_cm, k_cm = sb("la_q", [P, SEQ]), sb("la_k", [P, SEQ])
        e_q, r_q, e_k, r_k = (sb(f"la_er{n}", [P, SEQ]) for n in range(4))
        k_tm, v_tm = sb("la_ktm", [P, TILES, CH]), sb("la_vtm", [P, TILES, CH])
        ksum, kmean = sb("la_ksum", [P, 1]), sb("la_kmean", [P, HEADS])
        kv = [sb(f"la_kv{n}", [P, P]) for n in range(3)]
        den, z = sb("la_den", [P, TILES * HEADS]), sb("la_z", [P, TILES * HEADS])
        z_wide = sb("la_zw", [P, TILES * HEADS, HEAD])
        z_cm, attn = sb("la_zcm", [P, SEQ]), sb("la_attn", [P, SEQ])
        hidden = sb("la_hid", [P, HIDS, BANK])
        centre_w = sb("la_cw", [P, 2])
        out_cm = sb("la_out", [P, SEQ])

        edges = sig("la_edges")
        u_t, u_ready, x1_ready, x1_t = sig("la_ut"), sig("la_ur"), sig("la_x1r"), sig("la_x1t")
        xn_t, xn_ready = sig("la_xnt", 2), sig("la_xnr", 2)
        gate_mm, in_mm, gate_ready, xi_ready = sig("la_gm"), sig("la_im"), sig("la_gr"), sig("la_xir")
        conv_ready, v_ready = sig("la_cr"), sig("la_vr")
        qk_mm, qk_parts, qk_ready = sig("la_qkm", 2), sig("la_qkp", 4), sig("la_qkr", 2)
        kv_t, ktm_ready, vtm_ready = sig("la_kvt", 2), sig("la_ktr"), sig("la_vtr")
        km_ready, kv_mm, kv_ready = sig("la_kmr"), sig("la_kvm", 3), sig("la_kvr", 3)
        num_mm, den_mm, z_ready, z_t, zcm_ready = sig("la_nm"), sig("la_dm"), sig("la_zr"), sig("la_zt"), sig("la_zc")
        attn_ready, out_mm, x2_ready, x3_ready, x3_t = sig("la_ar"), sig("la_om"), sig("la_x2r"), sig("la_x3r"), sig("la_x3t")
        fc1_mm, fc1_ready, fc2_mm = sig("la_f1m", 8), sig("la_f1r", 8), sig("la_f2m", 2)
        o_ready, o_t, x_ready = sig("la_or"), sig("la_ot"), sig("la_xr")
        CHAIN = 15
        chain = sig("la_chain", CHAIN)

        ident = mat(m1, MATS1, "ident")

        with nc.Block() as block:

            @block.tensor
            def _(pe):
                with pe.Fori(0, BATCH) as b:
                    def transposes(out_tm, src, done):
                        for t in range(TILES):
                            last = nc.tensor.transpose(out_tm[:, t, :], src[:, t, :] if len(src.shape) == 3
                                                       else src[:, t * P:(t + 1) * P], ident)
                        last.then_inc(done.sem, 1)

                    def product(out, w, rhs, done, halves=HALVES):
                        for n in range(halves):
                            last = nc.tensor.matmul(out[:, n * BANK:(n + 1) * BANK], w,
                                                    rhs[:, n * BANK:(n + 1) * BANK], start=True, stop=True)
                        last.then_inc(done.sem, 1)

                    pe.wait_ge(ln.scaled.sem, ln.scaled.at(b, 1))
                    transposes(psA_tm, y_tm, u_t)
                    pe.wait_ge(x1_ready.sem, x1_ready.at(b))
                    transposes(psB_tm, x1, x1_t)
                    pe.wait_ge(ln.scaled.sem, ln.scaled.at(b, 2))
                    transposes(psA_tm, y_tm, xn_t)
                    pe.wait_ge(xn_ready.sem, xn_ready.at(b, 1))
                    product(psC, mat(m1, MATS1, "actp_w"), xn, gate_mm)
                    product(psD, mat(m1, MATS1, "in_w"), xn, in_mm)
                    pe.wait_ge(v_ready.sem, v_ready.at(b))
                    for n, dst in enumerate((psA, psB)):
                        product(dst, mat(m1, MATS1, "qk_w", n, CH), v_pad[:, 1:SEQ + 1], qk_mm)
                    transposes(psD_tm, v_pad[:, 1:SEQ + 1], kv_t)
                    pe.wait_ge(qk_ready.sem, qk_ready.at(b, 2))
                    pe.wait_ge(gate_ready.sem, gate_ready.at(b))
                    transposes(psC_tm, k_cm, kv_t)
                    pe.wait_ge(ktm_ready.sem, ktm_ready.at(b))
                    pe.wait_ge(vtm_ready.sem, vtm_ready.at(b))
                    for t in range(TILES):
                        last = nc.tensor.matmul(psA[:, 0:P], k_tm[:, t, :], v_tm[:, t, :],
                                                start=(t == 0), stop=(t == TILES - 1))
                    last.then_inc(kv_mm.sem, 1)
                    for n, name in enumerate(("rope_t", "rope")):
                        pe.wait_ge(kv_ready.sem, kv_ready.at(b, n + 1))
                        nc.tensor.matmul(psA[:, 0:P], mat(m1, MATS1, name), kv[n][:, :],
                                         start=True, stop=True).then_inc(kv_mm.sem, 1)
                    pe.wait_ge(km_ready.sem, km_ready.at(b))
                    for t in range(TILES):
                        last = nc.tensor.matmul(psC[:, t * HEADS:(t + 1) * HEADS], q_cm[:, t * P:(t + 1) * P],
                                                kmean[:, :], start=True, stop=True)
                    last.then_inc(den_mm.sem, 1)
                    pe.wait_ge(kv_ready.sem, kv_ready.at(b, 3))
                    product(psB, kv[2][:, :], q_cm, num_mm)
                    pe.wait_ge(z_ready.sem, z_ready.at(b))
                    z_flat = z_wide[:, :, :].rearrange("p a d -> p (a d)")
                    transposes(psD_tm, z_flat, z_t)
                    pe.wait_ge(attn_ready.sem, attn_ready.at(b))
                    product(psC, mat(m1, MATS1, "out_w"), attn, out_mm)
                    pe.wait_ge(x3_ready.sem, x3_ready.at(b))
                    transposes(psA_tm, x3, x3_t)
                    pe.wait_ge(ln.scaled.sem, ln.scaled.at(b, 3))
                    transposes(psB_tm, y_tm, xn_t)
                    pe.wait_ge(xn_ready.sem, xn_ready.at(b, 2))
                    for n in range(HALVES):
                        cols = slice(n * BANK, (n + 1) * BANK)
                        for k in range(HIDS):
                            if n:
                                pe.wait_ge(fc1_ready.sem, fc1_ready.at(b, k + 1))
                            nc.tensor.matmul(ps[:, 4 + k, :], mat(m1, MATS1, "fc1_w", k, P), xn[:, cols],
                                             start=True, stop=True).then_inc(fc1_mm.sem, 1)
                        for k in range(HIDS):
                            pe.wait_ge(fc1_ready.sem, fc1_ready.at(b, n * HIDS + k + 1))
                            last = nc.tensor.matmul(ps[:, n, :], mat(m1, MATS1, "fc2_w", k, CH), hidden[:, k, :],
                                                    start=(k == 0), stop=(k == HIDS - 1))
                        last.then_inc(fc2_mm.sem, 1)
                    pe.wait_ge(o_ready.sem, o_ready.at(b))
                    transposes(psB_tm, out_cm, o_t)
                    pe.wait_ge(x_ready.sem, x_ready.at(b))

            @block.scalar
            def _(act):
                with act.Fori(0, BATCH) as b:
                    def func(out, src, f, done, **more):
                        nc.scalar.activation(out, src, f, **more).then_inc(done.sem, 1)

                    ln.square(nc, act, b, 1)
                    ln.root(nc, act, b, 1)
                    act.wait_ge(u_t.sem, u_t.at(b))
                    func(u_pad[:, 1:SEQ + 1], psA, ACT.Copy, u_ready)
                    ln.square(nc, act, b, 2)
                    ln.root(nc, act, b, 2)
                    act.wait_ge(gate_mm.sem, gate_mm.at(b))
                    func(gate[:, :], psC, ACT.Silu, gate_ready, bias=vec(vecs, "actp_b"))
                    act.wait_ge(conv_ready.sem, conv_ready.at(b))
                    func(v_pad[:, 1:SEQ + 1], conv[:, :], ACT.Silu, v_ready, bias=vec(vecs, "dwc_b"))
                    for n, (src, e, r) in enumerate(((psA, e_q, r_q), (psB, e_k, r_k))):
                        act.wait_ge(qk_mm.sem, qk_mm.at(b, n + 1))
                        func(e[:, :], src, ACT.Exp, qk_parts, bias=vec(vecs, "qk_b", n))
                        func(r[:, :], src, ACT.Relu, qk_parts, bias=vec(vecs, "qk_b", n))
                    act.wait_ge(kv_t.sem, kv_t.at(b, 2))
                    func(k_tm[:, :, :], psC_tm, ACT.Copy, ktm_ready)
                    act.wait_ge(z_t.sem, z_t.at(b))
                    func(z_cm[:, :], psD, ACT.Copy, zcm_ready)
                    ln.square(nc, act, b, 3)
                    ln.root(nc, act, b, 3)
                    for n in range(HALVES):
                        if n:
                            act.wait_ge(fc2_mm.sem, fc2_mm.at(b, n))
                        for k in range(HIDS):
                            act.wait_ge(fc1_mm.sem, fc1_mm.at(b, n * HIDS + k + 1))
                            func(hidden[:, k, :], ps[:, 4 + k, :], ACT.Gelu, fc1_ready, bias=vec(vecs, "fc1_b", k))

            @block.vector
            def _(dve):
                for n, pad in enumerate((u_pad, x2_pad, xi_pad, v_pad)):
                    nc.vector.memset(pad[:, 0:1], 0.0).then_inc(edges.sem, 1)
                    nc.vector.memset(pad[:, SEQ + 1:SEQ + 2], 0.0).then_inc(edges.sem, 1)
                for n, name in enumerate(("cpe1_w", "cpe2_w")):
                    nc.vector.tensor_scalar(centre_w[:, n:n + 1], vec(vecs, name, 1), 1.0, None, ALU.add
                                            ).then_inc(edges.sem, 1)
                dve.wait_ge(edges.sem, 10)
                with dve.Fori(0, BATCH) as b:
                    made = [0]

                    def link(ins):
                        made[0] += 1
                        ins.then_inc(chain.sem, 1)
                        dve.wait_ge(chain.sem, chain.at(b, made[0]))

                    def tap(out, pad, k, w, acc):
                        return nc.vector.scalar_tensor_tensor(out=out, in0=pad[:, k:k + SEQ], scalar=w, in1=acc,
                                                              op0=ALU.mult, op1=ALU.add)

                    x_b = x[:, bass.ds(b * TILES, TILES), :]
                    ln.center(nc, dve, b, 1, x_b)
                    ln.variance(nc, dve, b, 1)
                    ln.scale(nc, dve, b, 1, y_tm[:, :, :])
                    dve.wait_ge(u_ready.sem, u_ready.at(b))
                    link(nc.vector.tensor_scalar(x1[:, :], u_pad[:, 1:SEQ + 1], centre_w[:, 0:1], vec(vecs, "cpe1_b"),
                                                 ALU.mult, ALU.add))
                    link(tap(x1[:, :], u_pad, 0, vec(vecs, "cpe1_w", 0), x1[:, :]))
                    tap(x1[:, :], u_pad, 2, vec(vecs, "cpe1_w", 2), x1[:, :]).then_inc(x1_ready.sem, 1)
                    dve.wait_ge(x1_t.sem, x1_t.at(b))
                    ln.center(nc, dve, b, 2, psB_tm)
                    ln.variance(nc, dve, b, 2)
                    ln.scale(nc, dve, b, 2, y_tm[:, :, :])
                    dve.wait_ge(xn_t.sem, xn_t.at(b, 1))
                    nc.vector.tensor_scalar(xn[:, :], psA, vec(vecs, "norm1_g"), vec(vecs, "norm1_b"),
                                            ALU.mult, ALU.add).then_inc(xn_ready.sem, 1)
                    dve.wait_ge(in_mm.sem, in_mm.at(b))
                    link(nc.vector.tensor_scalar(xi_pad[:, 1:SEQ + 1], psD, vec(vecs, "in_b"), None, ALU.add))
                    link(nc.vector.tensor_scalar(conv[:, :], xi_pad[:, 0:SEQ], vec(vecs, "dwc_w", 0), None, ALU.mult))
                    link(tap(conv[:, :], xi_pad, 1, vec(vecs, "dwc_w", 1), conv[:, :]))
                    tap(conv[:, :], xi_pad, 2, vec(vecs, "dwc_w", 2), conv[:, :]).then_inc(conv_ready.sem, 1)
                    for n, (e, r, out) in enumerate(((e_q, r_q, q_cm), (e_k, r_k, k_cm))):
                        dve.wait_ge(qk_parts.sem, qk_parts.at(b, 2 * n + 2))
                        nc.vector.scalar_tensor_tensor(out=out[:, :], in0=e[:, :], scalar=1.0, in1=r[:, :],
                                                       op0=ALU.min, op1=ALU.add).then_inc(qk_ready.sem, 1)
                    dve.wait_ge(kv_t.sem, kv_t.at(b, 1))
                    nc.vector.tensor_copy(v_tm[:, :, :], psD_tm).then_inc(vtm_ready.sem, 1)
                    dve.wait_ge(qk_ready.sem, qk_ready.at(b, 2))
                    link(nc.vector.reduce_sum(ksum[:, :], k_cm[:, :], axis=AX.X))
                    nc.vector.tensor_scalar(kmean[:, :], mat(m1, MATS1, "block16"), ksum[:, 0:1], 1.0 / SEQ,
                                            ALU.mult, ALU.mult).then_inc(km_ready.sem, 1)
                    dve.wait_ge(kv_mm.sem, kv_mm.at(b, 1))
                    nc.vector.scalar_tensor_tensor(out=kv[0][:, :], in0=psA[:, 0:P], scalar=1.0 / SEQ,
                                                   in1=mat(m1, MATS1, "block"), op0=ALU.mult, op1=ALU.mult
                                                   ).then_inc(kv_ready.sem, 1)
                    for n in (1, 2):
                        dve.wait_ge(kv_mm.sem, kv_mm.at(b, n + 1))
                        nc.vector.tensor_copy(kv[n][:, :], psA[:, 0:P]).then_inc(kv_ready.sem, 1)
                    dve.wait_ge(den_mm.sem, den_mm.at(b))
                    link(nc.vector.tensor_scalar(den[:, :], psC[:, 0:TILES * HEADS], 1e-6, None, ALU.add))
                    link(nc.vector.reciprocal(z[:, :], den[:, :]))
                    nc.vector.tensor_copy(z_wide[:, :, :], z[:, :].unsqueeze(2).broadcast_to([P, TILES * HEADS, HEAD])
                                          ).then_inc(z_ready.sem, 1)
                    dve.wait_ge(zcm_ready.sem, zcm_ready.at(b))
                    dve.wait_ge(num_mm.sem, num_mm.at(b))
                    link(nc.vector.tensor_tensor(attn[:, :], psB, z_cm[:, :], ALU.mult))
                    for k in range(3):
                        link(tap(attn[:, :], v_pad, k, vec(vecs, "lepe_w", k), attn[:, :]))
                    dve.wait_ge(gate_ready.sem, gate_ready.at(b))
                    nc.vector.scalar_tensor_tensor(out=attn[:, :], in0=attn[:, :], scalar=vec(vecs, "lepe_b"),
                                                   in1=gate[:, :], op0=ALU.add, op1=ALU.mult).then_inc(attn_ready.sem, 1)
                    dve.wait_ge(out_mm.sem, out_mm.at(b))
                    link(nc.vector.scalar_tensor_tensor(out=x2_pad[:, 1:SEQ + 1], in0=psC, scalar=vec(vecs, "out_b"),
                                                        in1=x1[:, :], op0=ALU.add, op1=ALU.add))
                    link(nc.vector.tensor_scalar(x3[:, :], x2_pad[:, 1:SEQ + 1], centre_w[:, 1:2], vec(vecs, "cpe2_b"),
                                                 ALU.mult, ALU.add))
                    link(tap(x3[:, :], x2_pad, 0, vec(vecs, "cpe2_w", 0), x3[:, :]))
                    tap(x3[:, :], x2_pad, 2, vec(vecs, "cpe2_w", 2), x3[:, :]).then_inc(x3_ready.sem, 1)
                    dve.wait_ge(x3_t.sem, x3_t.at(b))
                    ln.center(nc, dve, b, 3, psA_tm)
                    ln.variance(nc, dve, b, 3)
                    ln.scale(nc, dve, b, 3, y_tm[:, :, :])
                    dve.wait_ge(xn_t.sem, xn_t.at(b, 2))
                    nc.vector.tensor_scalar(xn[:, :], psB, vec(vecs, "norm2_g"), vec(vecs, "norm2_b"),
                                            ALU.mult, ALU.add).then_inc(xn_ready.sem, 1)
                    dve.wait_ge(fc2_mm.sem, fc2_mm.at(b, 2))
                    nc.vector.scalar_tensor_tensor(out=out_cm[:, :], in0=psA, scalar=vec(vecs, "fc2_b"), in1=x3[:, :],
                                                   op0=ALU.add, op1=ALU.add).then_inc(o_ready.sem, 1)
                    dve.wait_ge(o_t.sem, o_t.at(b))
                    nc.vector.tensor_tensor(x_b, psB_tm, x_b, ALU.add).then_inc(x_ready.sem, 1)
                    chain.used = made[0]
        assert chain.used == CHAIN, chain.used


def expert_mixture_block(nc, x, m2, pick, ident_b, m1, eps):
    UNITS = PAIRS + 1
    ALL = HALVES * UNITS
    with ExitStack() as ctx:
        def sb(name, shape, dt=F32):
            return ctx.enter_context(nc.sbuf_tensor(name, shape, dt))

        def sig(name, per=1):
            return Signal(ctx, nc, name, per)

        ps = ctx.enter_context(nc.psum_tensor("mx_ps", [P, 8, BANK], F32))
        low = ps[:, 0:2, :].rearrange("p a n -> p (a n)")
        high = ps[:, 6:8, :].rearrange("p a n -> p (a n)")
        low_tm, high_tm = (v.rearrange("p (t c) -> p t c", t=TILES) for v in (low, high))
        aff_ps = ps[:, 6, :].rearrange("p (t e) -> p t e", t=TILES)
        weights_hm_ps = ps[:, 2, :].bitcast(BF16)
        weights_lo_ps = ps[0:E0, 3, :].bitcast(BF16)

        buffers = (sb("mx_sums", [P, TILES]), sb("mx_cent", [P, TILES, CH]), sb("mx_sq", [P, TILES, CH]),
                   sb("mx_var", [P, TILES]), sb("mx_log", [P, TILES]), sb("mx_rstd", [P, TILES]), eps)
        ln = Norm(ctx, nc, "mx_ln", buffers, 1)
        y_tm = sb("mx_y", [P, TILES, CH])
        f_cm = sb("mx_f", [P, SEQ])
        biased, kept, sigm, rest = (sb(f"mx_r{n}", [P, TILES, E0]) for n in range(4))
        best = sb("mx_best", [P, TILES, 8])
        held = sb("mx_held", [P, 1])
        total, inverse = sb("mx_tot", [P, TILES]), sb("mx_inv", [P, TILES])
        hm = sb("mx_hm", [P, TILES, 2, E0], BF16)
        lo = sb("mx_lo", [P, TILES, E0], BF16)
        hm_cm, lo_cm = sb("mx_hmc", [P, SEQ], BF16), sb("mx_loc", [E0, SEQ], BF16)
        h, hw = sb("mx_h", [P, 3, BANK]), sb("mx_hw", [P, 3, BANK])
        out_cm = sb("mx_out", [P, SEQ])

        f_t, f_ready, aff_mm, sig_ready = sig("mx_ft"), sig("mx_fr"), sig("mx_am"), sig("mx_sr")
        best_ready, kept_ready = sig("mx_br", TILES), sig("mx_kr", TILES + 1)
        parts_ready, parts_t, weights_ready = sig("mx_pr"), sig("mx_pt"), sig("mx_wr")
        up_mm, pick_mm, silu_ready = sig("mx_up", ALL), sig("mx_pk", HALVES * PAIRS), sig("mx_sl", ALL)
        hw_ready, down_mm = sig("mx_hwr", ALL), sig("mx_dn", ALL)
        out_ready, out_t, x_ready = sig("mx_or", HALVES), sig("mx_ot"), sig("mx_xr")
        CHAIN = 12
        chain = sig("mx_chain", CHAIN)
        ident = mat(m1, MATS1, "ident")

        with nc.Block() as block:

            @block.tensor
            def _(pe):
                with pe.Fori(0, BATCH) as b:
                    pe.wait_ge(ln.scaled.sem, ln.scaled.at(b))
                    for t in range(TILES):
                        last = nc.tensor.transpose(low_tm[:, t, :], y_tm[:, t, :], ident)
                    last.then_inc(f_t.sem, 1)
                    pe.wait_ge(f_ready.sem, f_ready.at(b))
                    for t in range(TILES):
                        last = nc.tensor.matmul(aff_ps[:, t, :], f_cm[:, t * P:(t + 1) * P], mat(m2, MATS2, "cent"),
                                                start=True, stop=True)
                    last.then_inc(aff_mm.sem, 1)
                    pe.wait_ge(parts_ready.sem, parts_ready.at(b))
                    for t in range(TILES):
                        cols = slice(t * P, (t + 1) * P)
                        nc.tensor.transpose(weights_hm_ps[:, cols], hm[:, t, :, :].rearrange("p a e -> p (a e)"),
                                            ident_b[:, :])
                        last = nc.tensor.transpose(weights_lo_ps[:, cols], lo[:, t, :], ident_b[:, :])
                    last.then_inc(parts_t.sem, 1)
                    pe.wait_ge(weights_ready.sem, weights_ready.at(b))
                    for n in range(ALL + 1):
                        if n < ALL:
                            half, j = divmod(n, UNITS)
                            cols = slice(half * BANK, (half + 1) * BANK)
                            if n >= 2:
                                pe.wait_ge(silu_ready.sem, silu_ready.at(b, n - 1))
                            if j == 0:
                                nc.tensor.matmul(ps[0:F0, 2 + n % 2, :], mat(m2, MATS2, "shared_up"), f_cm[:, cols],
                                                 start=True, stop=True).then_inc(up_mm.sem, 1)
                            else:
                                nc.tensor.matmul(ps[:, 2 + n % 2, :], mat(m2, MATS2, "up", j - 1, P), f_cm[:, cols],
                                                 start=True, stop=True).then_inc(up_mm.sem, 1)
                                if n >= 2:
                                    pe.wait_ge(hw_ready.sem, hw_ready.at(b, n - 1))
                                nc.tensor.matmul(ps[:, 4 + n % 2, :], pick[:, (j - 1) * P:j * P], hm_cm[:, cols],
                                                 start=True, stop=False)
                                nc.tensor.matmul(ps[:, 4 + n % 2, :], pick[0:E0, (j - 1) * P:j * P], lo_cm[:, cols],
                                                 start=False, stop=True).then_inc(pick_mm.sem, 1)
                        if n:
                            half, j = divmod(n - 1, UNITS)
                            pe.wait_ge(hw_ready.sem, hw_ready.at(b, n))
                            if j == 0:
                                nc.tensor.matmul(ps[:, half, :], mat(m2, MATS2, "shared_down", rows=F0),
                                                 hw[0:F0, (n - 1) % 3, :], start=True, stop=False
                                                 ).then_inc(down_mm.sem, 1)
                            else:
                                nc.tensor.matmul(ps[:, half, :], mat(m2, MATS2, "down", j - 1, CH),
                                                 hw[:, (n - 1) % 3, :], start=False, stop=(j == PAIRS)
                                                 ).then_inc(down_mm.sem, 1)
                    pe.wait_ge(out_ready.sem, out_ready.at(b, HALVES))
                    for t in range(TILES):
                        last = nc.tensor.transpose(high_tm[:, t, :], out_cm[:, t * P:(t + 1) * P], ident)
                    last.then_inc(out_t.sem, 1)
                    pe.wait_ge(x_ready.sem, x_ready.at(b))

            @block.scalar
            def _(act):
                with act.Fori(0, BATCH) as b:
                    ln.square(nc, act, b, 1)
                    ln.root(nc, act, b, 1)
                    act.wait_ge(f_t.sem, f_t.at(b))
                    nc.scalar.activation(f_cm[:, :], low, ACT.Copy).then_inc(f_ready.sem, 1)
                    act.wait_ge(aff_mm.sem, aff_mm.at(b))
                    nc.scalar.activation(sigm[:, :, :], aff_ps, ACT.Sigmoid).then_inc(sig_ready.sem, 1)
                    for n in range(ALL):
                        half, j = divmod(n, UNITS)
                        rows = P if j else F0
                        act.wait_ge(up_mm.sem, up_mm.at(b, n + 1))
                        if n >= 3:
                            act.wait_ge(hw_ready.sem, hw_ready.at(b, n - 2))
                        nc.scalar.activation(h[0:rows, n % 3, :], ps[0:rows, 2 + n % 2, :], ACT.Silu
                                             ).then_inc(silu_ready.sem, 1)
                        if j == UNITS - 1:
                            act.wait_ge(down_mm.sem, down_mm.at(b, n + 1))
                            nc.scalar.activation(out_cm[:, half * BANK:(half + 1) * BANK], ps[:, half, :], ACT.Copy
                                                 ).then_inc(out_ready.sem, 1)

            @block.vector
            def _(dve):
                with dve.Fori(0, BATCH) as b:
                    made = [0]

                    def link(ins):
                        made[0] += 1
                        ins.then_inc(chain.sem, 1)
                        dve.wait_ge(chain.sem, chain.at(b, made[0]))

                    x_b = x[:, bass.ds(b * TILES, TILES), :]
                    ln.center(nc, dve, b, 1, x_b)
                    ln.variance(nc, dve, b, 1)
                    ln.scale(nc, dve, b, 1, y_tm[:, :, :])
                    dve.wait_ge(aff_mm.sem, aff_mm.at(b))
                    dve.wait_ge(sig_ready.sem, sig_ready.at(b))
                    link(nc.vector.tensor_tensor(biased[:, :, :], aff_ps,
                                                 mat(m2, MATS2, "bias").unsqueeze(1).broadcast_to([P, TILES, E0]),
                                                 ALU.add))
                    nc.vector.memset(held[:, :], 0.0)
                    for t in range(TILES):
                        nc.vector.max(best[:, t, :], biased[:, t, :]).then_inc(best_ready.sem, 1)
                    dve.wait_ge(best_ready.sem, best_ready.at(b, TILES))
                    nc.vector.memset(held[:, :], 0.0).then_inc(kept_ready.sem, 1)
                    for t in range(TILES):
                        nc.vector.match_replace(kept[:, t, :], best[:, t, :], biased[:, t, :], -3.0e38
                                                ).then_inc(kept_ready.sem, 1)
                    dve.wait_ge(kept_ready.sem, kept_ready.at(b, TILES + 1))
                    link(nc.vector.tensor_tensor(rest[:, :, :], kept[:, :, :], biased[:, :, :], ALU.not_equal))
                    link(nc.vector.tensor_tensor(rest[:, :, :], rest[:, :, :], sigm[:, :, :], ALU.mult))
                    link(nc.vector.reduce_sum(total[:, :], rest[:, :, :], axis=AX.X))
                    link(nc.vector.tensor_scalar(total[:, :], total[:, :], 1e-8, None, ALU.add))
                    link(nc.vector.reciprocal(inverse[:, :], total[:, :]))
                    link(nc.vector.tensor_tensor(rest[:, :, :], rest[:, :, :],
                                                 inverse[:, :].unsqueeze(2).broadcast_to([P, TILES, E0]), ALU.mult))
                    for part in (hm[:, :, 0, :], hm[:, :, 1, :]):
                        link(nc.vector.tensor_copy(part, rest[:, :, :]))
                        link(nc.vector.tensor_tensor(rest[:, :, :], rest[:, :, :], part, ALU.subtract))
                    nc.vector.tensor_copy(lo[:, :, :], rest[:, :, :]).then_inc(parts_ready.sem, 1)
                    dve.wait_ge(parts_t.sem, parts_t.at(b))
                    link(nc.vector.tensor_copy(hm_cm[:, :], weights_hm_ps))
                    nc.vector.tensor_copy(lo_cm[:, :], weights_lo_ps).then_inc(weights_ready.sem, 1)
                    for n in range(ALL):
                        half, j = divmod(n, UNITS)
                        dve.wait_ge(silu_ready.sem, silu_ready.at(b, n + 1))
                        if n >= 3:
                            dve.wait_ge(down_mm.sem, down_mm.at(b, n - 2))
                        if j == 0:
                            nc.vector.tensor_copy(hw[0:F0, n % 3, :], h[0:F0, n % 3, :]).then_inc(hw_ready.sem, 1)
                        else:
                            dve.wait_ge(pick_mm.sem, pick_mm.at(b, half * PAIRS + j))
                            nc.vector.tensor_tensor(hw[:, n % 3, :], ps[:, 4 + n % 2, :], h[:, n % 3, :], ALU.mult
                                                    ).then_inc(hw_ready.sem, 1)
                    dve.wait_ge(out_t.sem, out_t.at(b))
                    nc.vector.tensor_tensor(x_b, high_tm, x_b, ALU.add).then_inc(x_ready.sem, 1)
                    chain.used = made[0]
        assert chain.used == CHAIN, chain.used


ENTROPY_POLY = (-0.037, 0.481, -2.3, 4.917, -1.791)
PARTS = 3
STACK = PARTS * PARTS * HEAD
ROWS2 = STACK + PARTS
VW = 32
GROUP = 4
UNITS1 = HEADS * TILES
PACKS = [(0,), (1, 7), (2, 6), (3, 5), (4,)]
UNITS2 = HEADS * len(PACKS)


def pieces(pack, edge_of_query):
    out, at = [], 0
    for j in pack:
        q = j * P
        while q < SEQ:
            w = min(SEQ - q, BANK - at % BANK)
            if edge_of_query:
                w = min(w, BANK - q % BANK)
            out.append((j, at, q, w))
            at, q = at + w, q + w
    return out


def softmax_attention_block(nc, x, m3, masks, ident_b, m1, eps):
    with ExitStack() as ctx:
        def sb(name, shape, dt=F32):
            return ctx.enter_context(nc.sbuf_tensor(name, shape, dt))

        def sig(name, per=1):
            return Signal(ctx, nc, name, per)

        ps = ctx.enter_context(nc.psum_tensor("sa_ps", [P, 8, BANK], F32))

        def slot(k):
            return ps[:, 2 * k:2 * k + 2, :].rearrange("p a n -> p (a n)")

        def tiles_of(flat):
            return flat.rearrange("p (t c) -> p t c", t=TILES)

        buffers = (sb("sa_sums", [P, TILES]), sb("sa_cent", [P, TILES, CH]), sb("sa_sq", [P, TILES, CH]),
                   sb("sa_var", [P, TILES]), sb("sa_log", [P, TILES]), sb("sa_rstd", [P, TILES]), eps)
        ln = Norm(ctx, nc, "sa_ln", buffers, 1)
        y_tm = sb("sa_y", [P, TILES, CH])
        a_cm = sb("sa_a", [P, SEQ])
        q_cm = sb("sa_q", [P, SEQ])
        left = buffers[2][:, :, :].rearrange("p t c -> p (t c)")
        acc_sb = buffers[1][:, :, :].rearrange("p t c -> p (t c)")
        k_cm = y_tm[:, :, :].rearrange("p t c -> p (t c)")
        att_tm = y_tm[:, :, :].rearrange("p t (h d) -> p t h d", h=HEADS)
        parts = [sb(f"sa_parts{n}", [P, PARTS, SEQ], BF16) for n in range(2)]
        shift_parts = parts[1][0:HEADS, :, :]
        q_stack, k_stack, q2_stack = (sb(f"sa_{n}s", [ROWS2, HEADS, SEQ], BF16) for n in ("q", "k", "q2"))
        values = sb("sa_v", [P, TILES, HEADS, VW])
        nmax, sums, floor, prod = (sb(f"sa_{n}", [P, TILES, HEADS]) for n in ("nmax", "sum", "floor", "prod"))
        ent, poly, beta, log_sum = (sb(f"sa_{n}", [P, TILES, HEADS]) for n in ("ent", "poly", "beta", "lsum"))
        beta_hm, shift_hm = sb("sa_bh", [HEADS, SEQ]), sb("sa_sh", [HEADS, SEQ])
        e, lg = sb("sa_e", [P, 3, SEQ]), sb("sa_lg", [P, 2, SEQ])
        p_t = e
        inv = sb("sa_inv", [P, TILES, GROUP])
        spill = [nc.dram_tensor(f"sa_spill{n}", [PARTS, P, SEQ], BF16).ap() for n in range(3)]
        spill_shift = nc.dram_tensor("sa_spill_shift", [PARTS, HEADS, SEQ], BF16).ap()

        ready = sig("sa_const")
        a_t, a_ready, qkv_mm, qk_ready, v_ready = sig("sa_at"), sig("sa_ar"), sig("sa_qkv", 3), sig("sa_qkr", 2), sig("sa_vr")
        split = sig("sa_split", 2)
        spilled, stacked = sig("sa_spd", 32), sig("sa_std", 16 * 18)
        s_mm, max_ready, exp_ready = sig("sa_smm", UNITS1), sig("sa_mx", UNITS1), sig("sa_ex", UNITS1)
        floor_ready, log_ready, prod_ready = sig("sa_fl", UNITS1), sig("sa_lgr", UNITS1), sig("sa_pr", UNITS1)
        lsum_ready, beta_ready, beta_t = sig("sa_lsr"), sig("sa_br"), sig("sa_bt", 2)
        beta_copied, beta_wide = sig("sa_bc", 2), sig("sa_bw")
        split2, spilled2, stacked2 = sig("sa_split2", 2), sig("sa_spd2", 32), sig("sa_std2", 16 * 12)
        s2_mm, exp2_ready, pv_mm = sig("sa_s2"), sig("sa_e2"), sig("sa_pv")
        s2_mm.per = exp2_ready.per = pv_mm.per = UNITS2
        GROUPS = HEADS // GROUP
        acc_copied, acc_t, att_ready = sig("sa_acc_c", GROUPS), sig("sa_acc_t", GROUPS), sig("sa_attr", GROUPS)
        att_t, att_copied, o_mm, x_ready = sig("sa_att_t"), sig("sa_att_c"), sig("sa_o"), sig("sa_xr")
        CHAIN = 33
        chain = sig("sa_chain", CHAIN)
        ident = mat(m1, MATS1, "ident")
        mask_q, mask_k = masks[:, 0:P], masks[:, P:2 * P]

        with nc.Block() as block:

            @block.sync
            def _(sp):
                sp.wait_ge(ready.sem, 4)
                with sp.Fori(0, BATCH) as b:
                    for n in range(2):
                        sp.wait_ge(split.sem, split.at(b, n + 1))
                        sp.dma_start(spill[n].rearrange("a p n -> p a n"), parts[n][:, :, :]).then_inc(spilled.sem, 16)
                    for n, stack in enumerate((q_stack, k_stack)):
                        if n == 0:
                            sp.wait_ge(spilled.sem, spilled.at(b, 32))
                        for a in range(PARTS):
                            for c in range(PARTS):
                                r = (a * PARTS + c) * HEAD
                                src = spill[n][a if n == 0 else c].rearrange("(h d) n -> d h n", d=HEAD)
                                sp.dma_start(stack[r:r + HEAD, :, :], src).then_inc(stacked.sem, 16)
                    sp.wait_ge(split2.sem, split2.at(b, 1))
                    sp.dma_start(spill_shift.rearrange("a h n -> h a n"), shift_parts).then_inc(spilled2.sem, 16)
                    sp.wait_ge(split2.sem, split2.at(b, 2))
                    sp.dma_start(spill[2].rearrange("a p n -> p a n"), parts[0][:, :, :]).then_inc(spilled2.sem, 16)
                    sp.wait_ge(spilled2.sem, spilled2.at(b, 32))
                    for a in range(PARTS):
                        for c in range(PARTS):
                            r = (a * PARTS + c) * HEAD
                            sp.dma_start(q2_stack[r:r + HEAD, :, :], spill[2][a].rearrange("(h d) n -> d h n", d=HEAD)
                                         ).then_inc(stacked2.sem, 16)
                        sp.dma_start(q2_stack[STACK + a:STACK + a + 1, :, :], spill_shift[a:a + 1, :, :]
                                     ).then_inc(stacked2.sem, 16)

            @block.tensor
            def _(pe):
                pe.wait_ge(ready.sem, 4)
                with pe.Fori(0, BATCH) as b:
                    pe.wait_ge(ln.scaled.sem, ln.scaled.at(b))
                    for t in range(TILES):
                        last = nc.tensor.transpose(tiles_of(slot(0))[:, t, :], y_tm[:, t, :], ident)
                    last.then_inc(a_t.sem, 1)
                    pe.wait_ge(a_ready.sem, a_ready.at(b))
                    for k, name in enumerate(("wq", "wk")):
                        for n in range(HALVES):
                            cols = slice(n * BANK, (n + 1) * BANK)
                            last = nc.tensor.matmul(slot(1 + k)[:, cols], mat(m3, MATS3, name), a_cm[:, cols],
                                                    start=True, stop=True)
                        last.then_inc(qkv_mm.sem, 1)
                    for t in range(TILES):
                        last = nc.tensor.matmul(tiles_of(slot(3))[:, t, :], a_cm[:, t * P:(t + 1) * P],
                                                mat(m3, MATS3, "wv"), start=True, stop=True)
                    last.then_inc(qkv_mm.sem, 1)
                    pe.wait_ge(qk_ready.sem, qk_ready.at(b, 2))
                    pe.wait_ge(stacked.sem, stacked.at(b, 16 * 18))
                    for u in range(UNITS1):
                        h, i = divmod(u, TILES)
                        out = slot(u % 3)
                        if u >= 3:
                            pe.wait_ge(exp_ready.sem, exp_ready.at(b, u - 2))
                        keys = (i + 1) * P
                        for c in range(0, keys, BANK):
                            w = min(BANK, keys - c)
                            own = i * P < c + w
                            last = nc.tensor.matmul(out[:, c:c + w], q_stack[0:STACK, h, i * P:(i + 1) * P],
                                                    k_stack[0:STACK, h, c:c + w], start=True, stop=not own)
                        last = nc.tensor.matmul(out[:, i * P:keys], ident_b[:, :], mask_q, start=False, stop=True)
                        last.then_inc(s_mm.sem, 1)
                    pe.wait_ge(beta_ready.sem, beta_ready.at(b))
                    for n, src in enumerate((nmax, beta)):
                        for t in range(TILES):
                            last = nc.tensor.transpose(slot(n)[0:HEADS, t * P:(t + 1) * P], src[:, t, :], ident)
                        last.then_inc(beta_t.sem, 1)
                    pe.wait_ge(beta_copied.sem, beta_copied.at(b, 2))
                    for n in range(HALVES):
                        cols = slice(n * BANK, (n + 1) * BANK)
                        last = nc.tensor.matmul(slot(2)[:, cols], mat(m3, MATS3, "spread", rows=HEADS),
                                                beta_hm[:, cols], start=True, stop=True)
                    last.then_inc(beta_wide.sem, 1)
                    pe.wait_ge(split2.sem, split2.at(b, 2))
                    pe.wait_ge(stacked2.sem, stacked2.at(b, 16 * 12))
                    for v in range(UNITS2 + 1):
                        if v < UNITS2:
                            h, s = divmod(v, len(PACKS))
                            out = slot(v % 3)
                            if v >= 3:
                                pe.wait_ge(exp2_ready.sem, exp2_ready.at(b, v - 2))
                            for j, at, q, w in pieces(PACKS[s], False):
                                own = q == j * P
                                last = nc.tensor.matmul(out[:, at:at + w], k_stack[:, h, j * P:(j + 1) * P],
                                                        q2_stack[:, h, q:q + w], start=True, stop=not own)
                                if own:
                                    last = nc.tensor.matmul(out[:, at:at + P], ident_b[:, :], mask_k,
                                                            start=False, stop=True)
                            last.then_inc(s2_mm.sem, 1)
                        if v:
                            h, s = divmod(v - 1, len(PACKS))
                            g, rows = h // GROUP, slice(h % GROUP * VW, h % GROUP * VW + VW)
                            if s == 0 and h % GROUP == 0 and g:
                                pe.wait_ge(att_ready.sem, att_ready.at(b, g))
                            pe.wait_ge(exp2_ready.sem, exp2_ready.at(b, v))
                            for j, at, q, w in pieces(PACKS[s], True):
                                last = nc.tensor.matmul(slot(3)[rows, q:q + w], values[:, j, h, :],
                                                        p_t[:, (v - 1) % 3, at:at + w], start=(j == 0),
                                                        stop=(s == len(PACKS) - 1), skip_group_check=True)
                            last.then_inc(pv_mm.sem, 1)
                            if s == len(PACKS) - 1 and h % GROUP == GROUP - 1:
                                pe.wait_ge(acc_copied.sem, acc_copied.at(b, g + 1))
                                for t in range(TILES):
                                    last = nc.tensor.transpose(tiles_of(slot(3))[:, t, :], acc_sb[:, t * P:(t + 1) * P],
                                                               ident)
                                last.then_inc(acc_t.sem, 1)
                    pe.wait_ge(att_ready.sem, att_ready.at(b, GROUPS))
                    for t in range(TILES):
                        last = nc.tensor.transpose(slot(0)[:, t * P:(t + 1) * P],
                                                   att_tm[:, t, :, :].rearrange("p h d -> p (h d)"), ident)
                    last.then_inc(att_t.sem, 1)
                    pe.wait_ge(att_copied.sem, att_copied.at(b))
                    for t in range(TILES):
                        last = nc.tensor.matmul(tiles_of(slot(1))[:, t, :], a_cm[:, t * P:(t + 1) * P],
                                                mat(m3, MATS3, "wo"), start=True, stop=True)
                    last.then_inc(o_mm.sem, 1)
                    pe.wait_ge(x_ready.sem, x_ready.at(b))

            @block.scalar
            def _(act):
                nc.scalar.preload_act_table_set("natural_log_exp_and_others")
                with act.Fori(0, BATCH) as b:
                    ln.square(nc, act, b, 1)
                    ln.root(nc, act, b, 1, load=False)
                    act.wait_ge(a_t.sem, a_t.at(b))
                    nc.scalar.activation(a_cm[:, :], slot(0), ACT.Copy).then_inc(a_ready.sem, 1)
                    for n, (dst, scale) in enumerate(((q_cm[:, :], HEAD ** -0.5), (k_cm, 1.0))):
                        act.wait_ge(qkv_mm.sem, qkv_mm.at(b, n + 1))
                        nc.scalar.activation(dst, slot(1 + n), ACT.Copy, scale=scale).then_inc(qk_ready.sem, 1)
                    act.wait_ge(qkv_mm.sem, qkv_mm.at(b, 3))
                    nc.scalar.activation(values[:, :, :, 0:HEAD],
                                         slot(3).rearrange("p (t h d) -> p t h d", t=TILES, h=HEADS), ACT.Copy
                                         ).then_inc(v_ready.sem, 1)
                    for u in range(UNITS1 + 1):
                        if u < UNITS1:
                            h, i = divmod(u, TILES)
                            act.wait_ge(max_ready.sem, max_ready.at(b, u + 1))
                            if u >= 3:
                                act.wait_ge(prod_ready.sem, prod_ready.at(b, u - 2))
                            nc.scalar.activation(e[:, u % 3, 0:(i + 1) * P], slot(u % 3)[:, 0:(i + 1) * P], ACT.Exp,
                                                 bias=nmax[:, i, h:h + 1], accum_out=sums[:, i, h:h + 1]
                                                 ).then_inc(exp_ready.sem, 1)
                        if u:
                            h, i = divmod(u - 1, TILES)
                            act.wait_ge(floor_ready.sem, floor_ready.at(b, u))
                            nc.scalar.activation(lg[:, (u - 1) % 2, 0:(i + 1) * P], e[:, (u - 1) % 3, 0:(i + 1) * P],
                                                 ACT.Ln, bias=floor[:, i, h:h + 1]).then_inc(log_ready.sem, 1)
                    act.wait_ge(exp_ready.sem, exp_ready.at(b, UNITS1))
                    nc.scalar.activation(log_sum[:, :, :], sums[:, :, :], ACT.Ln).then_inc(lsum_ready.sem, 1)
                    for n, dst in enumerate((shift_hm, beta_hm)):
                        act.wait_ge(beta_t.sem, beta_t.at(b, n + 1))
                        nc.scalar.activation(dst[:, :], slot(n)[0:HEADS, :], ACT.Copy).then_inc(beta_copied.sem, 1)
                    for v in range(UNITS2):
                        h, s = divmod(v, len(PACKS))
                        w = sum(SEQ - j * P for j in PACKS[s])
                        act.wait_ge(s2_mm.sem, s2_mm.at(b, v + 1))
                        if v >= 3:
                            act.wait_ge(pv_mm.sem, pv_mm.at(b, v - 2))
                        nc.scalar.activation(p_t[:, v % 3, 0:w], slot(v % 3)[:, 0:w], ACT.Exp
                                             ).then_inc(exp2_ready.sem, 1)
                    act.wait_ge(att_t.sem, att_t.at(b))
                    nc.scalar.activation(a_cm[:, :], slot(0), ACT.Copy).then_inc(att_copied.sem, 1)

            @block.vector
            def _(dve):
                nc.vector.memset(values[:, :, :, :], 0.0).then_inc(ready.sem, 1)
                nc.vector.memset(k_stack[64:ROWS2, :, :], 1.0).then_inc(ready.sem, 1)
                nc.vector.memset(q2_stack[64:ROWS2, :, :], 0.0).then_inc(ready.sem, 1)
                dve.wait_ge(ready.sem, 3)
                nc.vector.memset(values[:, :, :, HEAD:HEAD + 1], 1.0).then_inc(ready.sem, 1)
                dve.wait_ge(ready.sem, 4)
                with dve.Fori(0, BATCH) as b:
                    made = [0]

                    def link(ins):
                        made[0] += 1
                        ins.then_inc(chain.sem, 1)
                        dve.wait_ge(chain.sem, chain.at(b, made[0]))

                    def split_up(src, rest, out, done):
                        link(nc.vector.tensor_copy(out[:, 0, :], src))
                        link(nc.vector.tensor_tensor(rest, src, out[:, 0, :], ALU.subtract))
                        link(nc.vector.tensor_copy(out[:, 1, :], rest))
                        link(nc.vector.tensor_tensor(rest, rest, out[:, 1, :], ALU.subtract))
                        nc.vector.tensor_copy(out[:, 2, :], rest).then_inc(done.sem, 1)

                    x_b = x[:, bass.ds(b * TILES, TILES), :]
                    ln.center(nc, dve, b, 1, x_b)
                    ln.variance(nc, dve, b, 1)
                    ln.scale(nc, dve, b, 1, y_tm[:, :, :])
                    for n, src in enumerate((q_cm[:, :], k_cm)):
                        dve.wait_ge(qk_ready.sem, qk_ready.at(b, n + 1))
                        split_up(src, left, parts[n], split)
                        dve.wait_ge(split.sem, split.at(b, n + 1))

                    def row_max(u):
                        h, i = divmod(u, TILES)
                        dve.wait_ge(s_mm.sem, s_mm.at(b, u + 1))
                        nc.vector.reduce_max(nmax[:, i, h:h + 1], slot(u % 3)[:, 0:(i + 1) * P], axis=AX.X, negate=True
                                             ).then_inc(max_ready.sem, 1)

                    row_max(0)
                    row_max(1)
                    for u in range(UNITS1 + 1):
                        if u + 2 < UNITS1:
                            row_max(u + 2)
                        if u < UNITS1:
                            h, i = divmod(u, TILES)
                            dve.wait_ge(exp_ready.sem, exp_ready.at(b, u + 1))
                            nc.vector.tensor_scalar(floor[:, i, h:h + 1], sums[:, i, h:h + 1], 1e-9, None, ALU.mult
                                                    ).then_inc(floor_ready.sem, 1)
                        if u:
                            h, i = divmod(u - 1, TILES)
                            dve.wait_ge(log_ready.sem, log_ready.at(b, u))
                            nc.vector.tensor_tensor_reduce(
                                out=lg[:, (u - 1) % 2, 0:(i + 1) * P], in0=e[:, (u - 1) % 3, 0:(i + 1) * P],
                                in1=lg[:, (u - 1) % 2, 0:(i + 1) * P], scale=1.0, scalar=0.0, op0=ALU.mult, op1=ALU.add,
                                accum_out=prod[:, i, h:h + 1]).then_inc(prod_ready.sem, 1)
                    dve.wait_ge(prod_ready.sem, prod_ready.at(b, UNITS1))
                    E, PO, BE, LS = ent[:, :, :], poly[:, :, :], beta[:, :, :], log_sum[:, :, :]
                    link(nc.vector.reciprocal(PO, sums[:, :, :]))
                    link(nc.vector.tensor_tensor(E, prod[:, :, :], PO, ALU.mult))
                    dve.wait_ge(lsum_ready.sem, lsum_ready.at(b))
                    link(nc.vector.tensor_tensor(E, LS, E, ALU.subtract))
                    link(nc.vector.tensor_scalar(PO, E, ENTROPY_POLY[0], None, ALU.mult))
                    for c in ENTROPY_POLY[1:4]:
                        link(nc.vector.scalar_tensor_tensor(out=PO, in0=PO, scalar=c, in1=E, op0=ALU.add, op1=ALU.mult))
                    link(nc.vector.tensor_scalar(PO, PO, ENTROPY_POLY[4], 1.0, ALU.add, ALU.max))
                    link(nc.vector.tensor_scalar(E, E, 0.5, None, ALU.is_gt))
                    link(nc.vector.scalar_tensor_tensor(out=PO, in0=PO, scalar=-1.0, in1=E, op0=ALU.add, op1=ALU.mult))
                    link(nc.vector.tensor_scalar(BE, PO, 1.0, None, ALU.add))
                    nc.vector.tensor_tensor(nmax[:, :, :], nmax[:, :, :], BE, ALU.mult).then_inc(beta_ready.sem, 1)
                    dve.wait_ge(beta_copied.sem, beta_copied.at(b, 1))
                    split_up(shift_hm[:, :], left[0:HEADS, :], shift_parts, split2)
                    dve.wait_ge(split2.sem, split2.at(b, 1))
                    dve.wait_ge(beta_wide.sem, beta_wide.at(b))
                    link(nc.vector.tensor_tensor(q_cm[:, :], slot(2), q_cm[:, :], ALU.mult))
                    split_up(q_cm[:, :], left, parts[0], split2)
                    for g in range(GROUPS):
                        dve.wait_ge(pv_mm.sem, pv_mm.at(b, (g + 1) * GROUP * len(PACKS)))
                        nc.vector.tensor_copy(acc_sb, slot(3)).then_inc(acc_copied.sem, 1)
                        dve.wait_ge(acc_t.sem, acc_t.at(b, g + 1))
                        acc_v = slot(3).rearrange("p (t g w) -> p t g w", t=TILES, g=GROUP)
                        link(nc.vector.reciprocal(inv[:, :, :], acc_v[:, :, :, HEAD]))
                        nc.vector.tensor_tensor(att_tm[:, :, g * GROUP:(g + 1) * GROUP, :], acc_v[:, :, :, 0:HEAD],
                                                inv[:, :, :].unsqueeze(3).broadcast_to([P, TILES, GROUP, HEAD]),
                                                ALU.mult).then_inc(att_ready.sem, 1)
                    link(nc.vector.tensor_tensor(x_b, x_b, mat(m3, MATS3, "bo").unsqueeze(1).broadcast_to([P, TILES, CH]),
                                                 ALU.add))
                    dve.wait_ge(o_mm.sem, o_mm.at(b))
                    nc.vector.tensor_tensor(x_b, tiles_of(slot(1)), x_b, ALU.add).then_inc(x_ready.sem, 1)
                    chain.used = made[0]
        assert chain.used == CHAIN, chain.used


E1 = 8
TOKENS = BATCH * SEQ
SHARE = TOKENS // E1
HID1 = 512
HIDS1 = HID1 // P
SHARE_TILES = SHARE // P
ROWS = 8
COPIES = P // ROWS
RUN = TOKENS // ROWS
HALF_KEY = 65536.0
STEPS = [COPIES ** k for k in (3, 2, 1, 0)]
TAKEN = -float(2 ** 34)


def scores_block(nc, x, feat, norm, scores, vecs, m1, m4, eps):
    with ExitStack() as ctx:
        def sb(name, shape, dt=F32):
            return ctx.enter_context(nc.sbuf_tensor(name, shape, dt))

        def sig(name, per=1):
            return Signal(ctx, nc, name, per)

        ps = ctx.enter_context(nc.psum_tensor("sc_ps", [P, 4, BANK], F32))
        low = ps[:, 0:2, :].rearrange("p a n -> p (a n)")
        low_tm = low.rearrange("p (t c) -> p t c", t=TILES)
        score_ps = ps[0:E1, 2:4, :].rearrange("p a n -> p (a n)")
        buffers = (sb("sc_sums", [P, TILES]), sb("sc_cent", [P, TILES, CH]), sb("sc_sq", [P, TILES, CH]),
                   sb("sc_var", [P, TILES]), sb("sc_log", [P, TILES]), sb("sc_rstd", [P, TILES]), eps)
        ln = Norm(ctx, nc, "sc_ln", buffers, 2)
        y_tm, n_cm, score_sb = sb("sc_y", [P, TILES, CH]), sb("sc_n", [P, SEQ]), sb("sc_s", [E1, SEQ])
        held, holding = sb("sc_held", [P, 1]), sig("sc_holding")
        n_t, n_ready, score_mm = sig("sc_nt"), sig("sc_nr"), sig("sc_mm")
        score_ready, kept, stored = sig("sc_sr"), sig("sc_kept"), sig("sc_st", 16)
        ident = mat(m1, MATS1, "ident")

        with nc.Block() as block:

            @block.sync
            def _(sp):
                with sp.Fori(0, BATCH) as b:
                    sp.wait_ge(score_ready.sem, score_ready.at(b))
                    sp.dma_start(scores[:, bass.ds(b * SEQ, SEQ)], score_sb[:, :]).then_inc(stored.sem, 16)
                sp.wait_ge(stored.sem, stored.at(BATCH - 1, 16))

            @block.tensor
            def _(pe):
                with pe.Fori(0, BATCH) as b:
                    pe.wait_ge(ln.scaled.sem, ln.scaled.at(b, 2))
                    for t in range(TILES):
                        last = nc.tensor.transpose(low_tm[:, t, :], y_tm[:, t, :], ident)
                    last.then_inc(n_t.sem, 1)
                    pe.wait_ge(n_ready.sem, n_ready.at(b))
                    for n in range(HALVES):
                        cols = slice(n * BANK, (n + 1) * BANK)
                        last = nc.tensor.matmul(score_ps[:, cols], mat(m4, MATS4, "cent1"), n_cm[:, cols],
                                                start=True, stop=True)
                    last.then_inc(score_mm.sem, 1)
                    pe.wait_ge(score_ready.sem, score_ready.at(b))

            @block.scalar
            def _(act):
                nc.scalar.preload_act_table_set("natural_log_exp_and_others")
                with act.Fori(0, BATCH) as b:
                    for k in (1, 2):
                        ln.square(nc, act, b, k)
                        ln.root(nc, act, b, k, load=False)
                    act.wait_ge(ln.scaled.sem, ln.scaled.at(b, 2))
                    nc.scalar.activation(norm[:, bass.ds(b * TILES, TILES), :], y_tm[:, :, :], ACT.Copy
                                         ).then_inc(kept.sem, 1)
                    act.wait_ge(score_mm.sem, score_mm.at(b))
                    nc.scalar.activation(score_sb[:, :], score_ps, ACT.Copy).then_inc(score_ready.sem, 1)
                    act.wait_ge(stored.sem, stored.at(b, 16))

            @block.vector
            def _(dve):
                with dve.Fori(0, BATCH) as b:
                    seq = bass.ds(b * TILES, TILES)
                    ln.center(nc, dve, b, 1, x[:, seq, :])
                    ln.variance(nc, dve, b, 1)
                    ln.scale(nc, dve, b, 1, feat[:, seq, :])
                    dve.wait_ge(ln.scaled.sem, ln.scaled.at(b, 1))
                    nc.vector.memset(held[:, :], 0.0).then_inc(holding.sem, 1)
                    ln.center(nc, dve, b, 2, feat[:, seq, :])
                    ln.variance(nc, dve, b, 2)
                    ln.scale(nc, dve, b, 2, y_tm[:, :, :])
                    dve.wait_ge(n_t.sem, n_t.at(b))
                    nc.vector.tensor_scalar(n_cm[:, :], low, vec(vecs, "ln_g"), vec(vecs, "ln_b"),
                                            ALU.mult, ALU.add).then_inc(n_ready.sem, 1)
                    dve.wait_ge(kept.sem, kept.at(b))


def assignment_block(nc, scores, keys_hi, keys_lo, places, index, m1, m4):
    with ExitStack() as ctx:
        def sb(name, shape, dt=F32):
            return ctx.enter_context(nc.sbuf_tensor(name, shape, dt))

        def sig(name, per=1):
            return Signal(ctx, nc, name, per)

        ps = ctx.enter_context(nc.psum_tensor("as_ps", [P, 3, BANK], F32))
        I32, U16 = mybir.dt.int32, mybir.dt.uint16
        WIDE = E1 * TOKENS // P
        bits, flip, key, half = (sb(f"as_b{n}", [P, WIDE], I32) for n in range(4))
        hi16, lo16 = sb("as_h16", [P, WIDE], U16), sb("as_l16", [P, WIDE], U16)
        hi, lo = sb("as_hi", [P, E1, RUN], U16), sb("as_lo", [P, E1, RUN], U16)
        penalty, value, low_value, hit, above, equal, chosen, order, place = (
            sb(f"as_v{n}", [P, RUN]) for n in range(9))
        ones = sb("as_ones", [P, RUN])
        base, thresh, count, passed, limit, rank0 = (sb(f"as_c{n}", [P, 1]) for n in range(6))
        by_copy, hits16 = sb("as_bc", [P, COPIES]), sb("as_h", [P, COPIES])
        two, both = sb("as_two", [P, 2]), sb("as_both", [P, 4])
        first = sb("as_first", [P, 1])
        place_rows = sb("as_pr", [TOKENS // P, P])

        loaded, split, stored, copied = sig("as_ld"), sig("as_sp"), sig("as_st"), sig("as_cp")
        CHAIN = 51
        chain = sig("as_chain", CHAIN)
        counted, count_mm = sig("as_ct", 2 * len(STEPS)), sig("as_cm", 2 * len(STEPS))
        sums_ready, sums_mm = sig("as_sr", 2), sig("as_sm", 2)
        placed, place_st, place_t, index_ready = sig("as_pl"), sig("as_ps"), sig("as_pt"), sig("as_ix")
        ident = mat(m1, MATS1, "ident")

        with nc.Block() as block:

            @block.sync
            def _(sp):
                flat = scores.rearrange("e n -> (e n)").rearrange("(p f) -> p f", p=P)
                sp.dma_start(bits[:, :], flat.bitcast(I32)).then_inc(loaded.sem, 16)
                sp.wait_ge(split.sem, 6)
                for dram, part in ((keys_hi, hi16), (keys_lo, lo16)):
                    sp.dma_start(dram.rearrange("e n -> (e n)").rearrange("(p f) -> p f", p=P), part[:, :]
                                 ).then_inc(stored.sem, 16)
                sp.wait_ge(stored.sem, 32)
                for dram, part in ((keys_hi, hi), (keys_lo, lo)):
                    for c in range(COPIES):
                        sp.dma_start(part[c * ROWS:(c + 1) * ROWS, :, :], dram.rearrange("e (r j) -> r e j", r=ROWS)
                                     ).then_inc(copied.sem, 16)
                sp.wait_ge(placed.sem, 1)
                sp.dma_start(places.rearrange("(r j) -> r j", r=ROWS), place[0:ROWS, :]).then_inc(place_st.sem, 16)
                sp.wait_ge(place_st.sem, 16)
                sp.dma_start(place_rows[:, :], places.rearrange("(t p) -> t p", p=P)).then_inc(place_st.sem, 16)

            @block.tensor
            def _(pe):
                with pe.Fori(0, E1) as e:
                    for k in range(2 * len(STEPS)):
                        pe.wait_ge(counted.sem, counted.at(e, k + 1))
                        nc.tensor.matmul(ps[:, 0, 0:COPIES], mat(m4, MATS4, "ones"), by_copy[:, :],
                                         start=True, stop=True).then_inc(count_mm.sem, 1)
                    for k in range(2):
                        pe.wait_ge(sums_ready.sem, sums_ready.at(e, k + 1))
                        nc.tensor.matmul(ps[:, 1, 0:2], mat(m4, MATS4, "same"), two[:, :], start=True, stop=True)
                        nc.tensor.matmul(ps[:, 1, 2:4], mat(m4, MATS4, "before"), two[:, :], start=True, stop=True
                                         ).then_inc(sums_mm.sem, 1)
                pe.wait_ge(place_st.sem, 32)
                rows = TOKENS // P
                nc.tensor.transpose(ps[:, 2, 0:rows], place_rows[:, :], mat(m1, MATS1, "ident", rows=rows)[:, 0:rows]
                                    ).then_inc(place_t.sem, 1)

            @block.vector
            def _(dve):
                n_split = [0]

                def step(ins):
                    n_split[0] += 1
                    ins.then_inc(split.sem, 1)
                    dve.wait_ge(split.sem, n_split[0])

                dve.wait_ge(loaded.sem, 16)
                step(nc.vector.tensor_scalar(flip[:, :], bits[:, :], 31, -2 ** 31, ALU.arith_shift_right, ALU.bitwise_or))
                step(nc.vector.tensor_tensor(key[:, :], bits[:, :], flip[:, :], ALU.bitwise_xor))
                step(nc.vector.tensor_scalar(half[:, :], key[:, :], 16, None, ALU.logical_shift_right))
                step(nc.vector.tensor_copy(hi16[:, :], half[:, :]))
                step(nc.vector.tensor_scalar(half[:, :], key[:, :], 0xFFFF, None, ALU.bitwise_and))
                step(nc.vector.tensor_copy(lo16[:, :], half[:, :]))
                step(nc.vector.memset(penalty[:, :], 0.0))
                step(nc.vector.memset(place[:, :], 0.0))
                step(nc.vector.memset(ones[:, :], 1.0))
                step(nc.vector.memset(first[:, :], -1.0))
                dve.wait_ge(copied.sem, 32 * COPIES)
                with dve.Fori(0, E1) as e:
                    made = [0]

                    def link(ins):
                        made[0] += 1
                        ins.then_inc(chain.sem, 1)
                        dve.wait_ge(chain.sem, chain.at(e, made[0]))

                    def search(v, turn):
                        scale = HALF_KEY if turn == 0 else 1.0
                        link(nc.vector.memset(base[:, :], 0.0))
                        for k, s in enumerate(STEPS):
                            link(nc.vector.tensor_tensor(thresh[:, :], base[:, :],
                                                         mat(m4, MATS4, "offsets", turn * len(STEPS) + k, 1), ALU.add))
                            link(nc.vector.tensor_scalar(hit[:, :], v, thresh[:, 0:1], 0.0, ALU.is_ge, ALU.add,
                                                         accum_out=count[:, :]))
                            nc.vector.tensor_scalar(by_copy[:, :], mat(m4, MATS4, "copies"), count[:, 0:1], None, ALU.mult
                                                    ).then_inc(counted.sem, 1)
                            dve.wait_ge(count_mm.sem, count_mm.at(e, turn * len(STEPS) + k + 1))
                            link(nc.vector.tensor_scalar(hits16[:, :], ps[:, 0, 0:COPIES], float(SHARE), 0.0, ALU.is_ge,
                                                         ALU.add, accum_out=passed[:, :]))
                            link(nc.vector.scalar_tensor_tensor(out=base[:, :], in0=passed[:, :], scalar=s * scale,
                                                                in1=base[:, :], op0=ALU.mult, op1=ALU.add))
                        link(nc.vector.tensor_scalar(base[:, :], base[:, :], -scale * sum(STEPS), None, ALU.add))

                    link(nc.vector.scalar_tensor_tensor(out=value[:, :], in0=hi[:, bass.ds(e, 1), :].squeeze(1),
                                                        scalar=HALF_KEY, in1=penalty[:, :], op0=ALU.mult, op1=ALU.add))
                    search(value[:, :], 0)
                    link(nc.vector.scalar_tensor_tensor(out=low_value[:, :], in0=value[:, :], scalar=base[:, 0:1],
                                                        in1=lo[:, bass.ds(e, 1), :].squeeze(1), op0=ALU.subtract,
                                                        op1=ALU.add))
                    search(low_value[:, :], 1)
                    link(nc.vector.tensor_scalar(above[:, :], low_value[:, :], base[:, 0:1], 0.0, ALU.is_gt, ALU.add,
                                                 accum_out=two[:, 0:1]))
                    link(nc.vector.tensor_scalar(equal[:, :], low_value[:, :], base[:, 0:1], 0.0, ALU.is_equal, ALU.add,
                                                 accum_out=two[:, 1:2]))
                    nc.vector.tensor_tensor_scan(order[:, :], ones[:, :], equal[:, :], 0.0, ALU.mult, ALU.add
                                                 ).then_inc(sums_ready.sem, 1)
                    dve.wait_ge(sums_mm.sem, sums_mm.at(e, 1))
                    link(nc.vector.tensor_copy(both[:, :], ps[:, 1, 0:4]))
                    link(nc.vector.tensor_tensor(limit[:, :], both[:, 0:1], both[:, 3:4], ALU.add))
                    link(nc.vector.tensor_scalar(limit[:, :], limit[:, :], -1.0, float(SHARE), ALU.mult, ALU.add))
                    link(nc.vector.scalar_tensor_tensor(out=chosen[:, :], in0=order[:, :], scalar=limit[:, 0:1],
                                                        in1=equal[:, :], op0=ALU.is_le, op1=ALU.mult))
                    link(nc.vector.tensor_tensor(chosen[:, :], chosen[:, :], above[:, :], ALU.add))
                    link(nc.vector.reduce_sum(two[:, 0:1], chosen[:, :], axis=AX.X))
                    nc.vector.tensor_tensor_scan(order[:, :], ones[:, :], chosen[:, :], first[:, 0:1], ALU.mult, ALU.add
                                                 ).then_inc(sums_ready.sem, 1)
                    link(nc.vector.scalar_tensor_tensor(out=penalty[:, :], in0=chosen[:, :], scalar=TAKEN,
                                                        in1=penalty[:, :], op0=ALU.mult, op1=ALU.add))
                    dve.wait_ge(sums_mm.sem, sums_mm.at(e, 2))
                    link(nc.vector.tensor_copy(rank0[:, :], ps[:, 1, 2:3]))
                    link(nc.vector.scalar_tensor_tensor(out=order[:, :], in0=order[:, :], scalar=rank0[:, 0:1],
                                                        in1=chosen[:, :], op0=ALU.add, op1=ALU.mult))
                    link(nc.vector.tensor_tensor(place[:, :], place[:, :], order[:, :], ALU.add))
                    link(nc.vector.tensor_scalar(first[:, :], first[:, :], float(SHARE), None, ALU.add))
                    chain.used = made[0]
                nc.vector.memset(count[:, :], 0.0).then_inc(placed.sem, 1)
                dve.wait_ge(place_t.sem, 1)
                nc.vector.tensor_copy(index[:, :], ps[:, 2, 0:TOKENS // P]).then_inc(index_ready.sem, 1)
                dve.wait_ge(index_ready.sem, 1)
        assert chain.used == CHAIN, chain.used


def balanced_experts_block(nc, x, feat, norm, index, routed, answers, w1_in, w2_in, vecs, m1):
    with ExitStack() as ctx:
        def sb(name, shape, dt=F32):
            return ctx.enter_context(nc.sbuf_tensor(name, shape, dt))

        def sig(name, per=1):
            return Signal(ctx, nc, name, per)

        ps = ctx.enter_context(nc.psum_tensor("be_ps", [P, 8, BANK], F32))
        w1, w2 = sb("be_w1", [P, 2, HID1]), sb("be_w2", [P, 2, HID1])
        rows = sb("be_rows", [P, 2, SHARE_TILES, CH])
        h_cm, hidden = sb("be_h", [P, SHARE]), sb("be_hid", [P, HIDS1, SHARE])
        o_cm, o_tm = sb("be_o", [P, SHARE]), sb("be_ot", [P, 2, SHARE_TILES, CH])
        back = sb("be_back", [P, TOKENS // P, CH])
        w_loaded, r_loaded = [sig(f"be_wl{n}") for n in range(2)], [sig(f"be_rl{n}") for n in range(2)]
        scattered, stored, gathered = sig("be_sc"), sig("be_so"), sig("be_ga")
        rows_t, h_ready, up_mm, hid_ready = sig("be_rt"), sig("be_hr"), sig("be_um"), sig("be_hd")
        down_mm, o_ready, o_t, ot_ready, sum_ready = sig("be_dm"), sig("be_or"), sig("be_tt"), sig("be_otr"), sig("be_x")
        ident = mat(m1, MATS1, "ident")
        routed_v = routed.rearrange("(e t p) c -> e p t c", t=SHARE_TILES, p=P)
        answers_v = answers.rearrange("(e t p) c -> e p t c", t=SHARE_TILES, p=P)

        with nc.Block() as block:

            @block.gpsimd
            def _(pool):
                for t in range(TOKENS // P):
                    pool.indirect_dma_start(routed, bass.IndirectOffsetOnAxis(ap=index[:, t:t + 1], axis=0),
                                            norm[:, t, :], None).then_inc(scattered.sem, 16)
                pool.wait_ge(stored.sem, 16 * E1)
                for t in range(TOKENS // P):
                    pool.indirect_dma_start(back[:, t, :], None, answers,
                                            bass.IndirectOffsetOnAxis(ap=index[:, t:t + 1], axis=0)
                                            ).then_inc(gathered.sem, 16)

            @block.sync
            def _(sp):
                for e in range(E1):
                    if e >= 2:
                        sp.wait_ge(down_mm.sem, e - 1)
                    sp.dma_start(w1[:, e % 2, :], w1_in[e]).then_inc(w_loaded[e % 2].sem, 16)
                    sp.dma_start(w2[:, e % 2, :], w2_in[e]).then_inc(w_loaded[e % 2].sem, 16)
                    if e == 0:
                        sp.wait_ge(scattered.sem, 16 * (TOKENS // P))
                    sp.dma_start(rows[:, e % 2, :, :], routed_v[e]).then_inc(r_loaded[e % 2].sem, 16)
                    if e:
                        sp.wait_ge(ot_ready.sem, e)
                        sp.dma_start(answers_v[e - 1], o_tm[:, (e - 1) % 2, :, :]).then_inc(stored.sem, 16)
                sp.wait_ge(ot_ready.sem, E1)
                sp.dma_start(answers_v[E1 - 1], o_tm[:, (E1 - 1) % 2, :, :]).then_inc(stored.sem, 16)

            @block.tensor
            def _(pe):
                for e in range(E1):
                    pe.wait_ge(r_loaded[e % 2].sem, 16 * (e // 2 + 1))
                    if e:
                        pe.wait_ge(h_ready.sem, e)
                    for t in range(SHARE_TILES):
                        last = nc.tensor.transpose(ps[:, 0, t * P:(t + 1) * P], rows[:, e % 2, t, :], ident)
                    last.then_inc(rows_t.sem, 1)
                    pe.wait_ge(h_ready.sem, e + 1)
                    pe.wait_ge(w_loaded[e % 2].sem, 32 * (e // 2 + 1))
                    for k in range(HIDS1):
                        if e:
                            pe.wait_ge(hid_ready.sem, (e - 1) * HIDS1 + k + 1)
                        nc.tensor.matmul(ps[:, 1 + k, :], w1[:, e % 2, k * P:(k + 1) * P], h_cm[:, :],
                                         start=True, stop=True).then_inc(up_mm.sem, 1)
                    if e:
                        pe.wait_ge(o_ready.sem, e)
                    for k in range(HIDS1):
                        pe.wait_ge(hid_ready.sem, e * HIDS1 + k + 1)
                        last = nc.tensor.matmul(ps[:, 5, :], w2[:, e % 2, k * P:(k + 1) * P], hidden[:, k, :],
                                                start=(k == 0), stop=(k == HIDS1 - 1))
                    last.then_inc(down_mm.sem, 1)
                    pe.wait_ge(o_ready.sem, e + 1)
                    if e:
                        pe.wait_ge(ot_ready.sem, e)
                    for t in range(SHARE_TILES):
                        last = nc.tensor.transpose(ps[:, 6, t * P:(t + 1) * P], o_cm[:, t * P:(t + 1) * P], ident)
                    last.then_inc(o_t.sem, 1)

            @block.scalar
            def _(act):
                for e in range(E1):
                    if e:
                        act.wait_ge(down_mm.sem, e)
                    for k in range(HIDS1):
                        act.wait_ge(up_mm.sem, e * HIDS1 + k + 1)
                        nc.scalar.activation(hidden[:, k, :], ps[:, 1 + k, :], ACT.Gelu_apprx_tanh,
                                             bias=vec(vecs, "b1", e * HIDS1 + k)).then_inc(hid_ready.sem, 1)

            @block.vector
            def _(dve):
                for e in range(E1):
                    dve.wait_ge(rows_t.sem, e + 1)
                    nc.vector.tensor_scalar(h_cm[:, :], ps[:, 0, :], vec(vecs, "ln_g"), vec(vecs, "ln_b"),
                                            ALU.mult, ALU.add).then_inc(h_ready.sem, 1)
                    dve.wait_ge(down_mm.sem, e + 1)
                    nc.vector.tensor_scalar(o_cm[:, :], ps[:, 5, :], vec(vecs, "b2", e), None, ALU.add
                                            ).then_inc(o_ready.sem, 1)
                    dve.wait_ge(o_t.sem, e + 1)
                    if e >= 2:
                        dve.wait_ge(stored.sem, 16 * (e - 1))
                    nc.vector.tensor_copy(o_tm[:, e % 2, :, :], ps[:, 6, :].rearrange("p (t c) -> p t c", c=CH)
                                          ).then_inc(ot_ready.sem, 1)
                nc.vector.tensor_tensor(x[:, :, :], x[:, :, :], feat[:, :, :], ALU.add).then_inc(sum_ready.sem, 1)
                dve.wait_ge(sum_ready.sem, 1)
                dve.wait_ge(gathered.sem, 16 * (TOKENS // P))
                nc.vector.tensor_tensor(x[:, :, :], x[:, :, :], back[:, :, :], ALU.add).then_inc(sum_ready.sem, 1)
                dve.wait_ge(sum_ready.sem, 2)


def program(nc, x_in, vecs_in, m1_in, m2_in, pick_in, m3_in, masks_in, m4_in, w1_in, w2_in, out, phases=4, start=0):
    with ExitStack() as ctx:
        def sb(name, shape, dt=F32):
            return ctx.enter_context(nc.sbuf_tensor(name, shape, dt))

        x = sb("x_res", [P, BATCH * TILES, CH])
        vecs = sb("vecs", [P, VECS["all"][1]])
        m1 = sb("m1", [P, MATS1["all"][1]])
        m3 = sb("m3", [P, MATS3["all"][1]])
        masks = sb("masks", [P, 2 * P], BF16)
        ident_b = sb("ident_b", [P, P], BF16)
        eps = sb("eps", [P, 1])
        x_view = x_in.rearrange("b (t p) c -> p (b t) c", p=P)
        Signal.live.clear()
        loaded = Signal(ctx, nc, "loaded")
        set_up = Signal(ctx, nc, "set_up")
        with nc.Block() as block:
            @block.sync
            def _(sp):
                sp.dma_start(x[:, :, :], x_view).then_inc(loaded.sem, 16)
                sp.dma_start(m1[:, :], m1_in).then_inc(loaded.sem, 16)
                sp.dma_start(m3[:, :], m3_in).then_inc(loaded.sem, 16)
                sp.dma_start(masks[:, :], masks_in).then_inc(loaded.sem, 16)
                sp.dma_start(vecs[:, :], vecs_in).then_inc(loaded.sem, 16)
                sp.wait_ge(loaded.sem, 80)

            @block.vector
            def _(dve):
                nc.vector.memset(eps[:, :], EPS).then_inc(set_up.sem, 1)
                dve.wait_ge(loaded.sem, 80)
                nc.vector.tensor_copy(ident_b[:, :], mat(m1, MATS1, "ident")).then_inc(set_up.sem, 1)
                dve.wait_ge(set_up.sem, 2)
        if phases >= 1 and start < 1:
            linear_attention_block(nc, x, vecs, m1, eps)
            retire(nc)
        if phases >= 2 and start < 2:
            with nc.sbuf_tensor("m2", [P, MATS2["all"][1]], F32) as m2, \
                    nc.sbuf_tensor("pick", [P, PAIRS * P], BF16) as pick:
                loaded2 = Signal(ctx, nc, "loaded2")
                with nc.Block() as block:
                    @block.sync
                    def _(sp):
                        sp.dma_start(m2[:, :], m2_in).then_inc(loaded2.sem, 16)
                        sp.dma_start(pick[:, :], pick_in).then_inc(loaded2.sem, 16)
                        sp.wait_ge(loaded2.sem, 32)
                expert_mixture_block(nc, x, m2, pick, ident_b, m1, eps)
        if phases >= 3 and start < 3:
            softmax_attention_block(nc, x, m3, masks, ident_b, m1, eps)
        if phases >= 4:
            scores = nc.dram_tensor("scores", [E1, TOKENS], F32).ap()
            keys_hi = nc.dram_tensor("keys_hi", [E1, TOKENS], mybir.dt.uint16).ap()
            keys_lo = nc.dram_tensor("keys_lo", [E1, TOKENS], mybir.dt.uint16).ap()
            places = nc.dram_tensor("places", [TOKENS], F32).ap()
            routed = nc.dram_tensor("routed", [TOKENS, CH], F32).ap()
            answers = nc.dram_tensor("answers", [TOKENS, CH], F32).ap()
            feat, norm = sb("feat", [P, TOKENS // P, CH]), sb("norm", [P, TOKENS // P, CH])
            index = sb("index", [P, TOKENS // P], mybir.dt.uint32)
            m4 = sb("m4", [P, MATS4["all"][1]])
            with nc.Block() as block:
                @block.sync
                def _(sp):
                    m4_loaded = Signal(ctx, nc, "m4_loaded")
                    sp.dma_start(m4[:, :], m4_in).then_inc(m4_loaded.sem, 16)
                    sp.wait_ge(m4_loaded.sem, 16)
            scores_block(nc, x, feat, norm, scores, vecs, m1, m4, eps)
            assignment_block(nc, scores, keys_hi, keys_lo, places, index, m1, m4)
            balanced_experts_block(nc, x, feat, norm, index, routed, answers, w1_in, w2_in, vecs, m1)
        stored = Signal(ctx, nc, "stored")
        with nc.Block() as block:
            @block.sync
            def _(sp):
                sp.dma_start(out.rearrange("b (t p) c -> p (b t) c", p=P), x[:, :, :]).then_inc(stored.sem, 16)
                sp.wait_ge(stored.sem, 16)


def constants():
    eye = np.eye(P, dtype=np.float32)
    pairs = CH // 2
    theta = (np.float32(1.0) / np.float32(10000.0) ** (np.arange(pairs, dtype=np.float32) / np.float32(pairs))).astype(np.float32)
    cos, sin = np.cos(theta), np.sin(theta)
    rope = np.zeros((P, P), np.float32)
    i = np.arange(pairs)
    rope[2 * i, 2 * i], rope[2 * i, 2 * i + 1] = cos, -sin
    rope[2 * i + 1, 2 * i], rope[2 * i + 1, 2 * i + 1] = sin, cos
    head = np.arange(P) // HEAD
    block = (head[:, None] == head[None, :]).astype(np.float32)
    block16 = (head[:, None] == np.arange(HEADS)[None, :]).astype(np.float32)
    expert = np.arange(P)[:, None, None] % E0
    owner = 2 * np.arange(PAIRS)[None, :, None] + np.arange(P)[None, None, :] // F0
    pick = (expert == owner).reshape(P, PAIRS * P).astype(mybir.dt.np(BF16))
    later = np.arange(P)[None, :] > np.arange(P)[:, None]
    masks = (np.concatenate([later, later.T], axis=1) * -3.0e38).astype(mybir.dt.np(BF16))
    copy, row = np.arange(P) // ROWS, np.arange(P) % ROWS
    same = copy[:, None] == copy[None, :]
    before = same & (row[:, None] < row[None, :])
    copies = copy[:, None] == np.arange(COPIES)[None, :]
    offsets = [scale * (copy * s - sum(STEPS[:k])) for scale in (HALF_KEY, 1.0) for k, s in enumerate(STEPS)]
    extra = {"ones": np.ones((P, P), np.float32), "same": same.astype(np.float32), "before": before.astype(np.float32),
             "copies": copies.astype(np.float32), "offsets": np.stack(offsets, 1).astype(np.float32)}
    return {**extra, "masks": masks, "pick": pick, "ident": eye, "rope": rope, "rope_t": np.ascontiguousarray(rope.T), "block": block, "block16": block16}


def layouts(inputs):
    a = {k: np.asarray(v) for k, v in inputs.items()}
    L = "L0_attn_"

    def columns(v, k):
        return np.ascontiguousarray(v.reshape(k, P).T)

    parts = []
    for n in VECS:
        if n == "all":
            continue
        if n in ("cpe1_w", "dwc_w", "lepe_w", "cpe2_w"):
            parts.append(a[L + n].reshape(P, 3))
        elif n in ("ln_g", "ln_b"):
            parts.append(columns(a["L1_ffn_" + n], 1))
        elif n in ("b1", "b2"):
            v = a["L1_ffn_" + n]
            parts.append(columns(v, v.size // P))
        else:
            v = a[L + n]
            parts.append(columns(v, v.size // P))
    vecs = np.concatenate(parts, axis=1)
    c = constants()
    m1 = np.concatenate([c["ident"], c["rope"], c["rope_t"], c["block"], c["block16"], a[L + "actp_w"], a[L + "in_w"],
                         a[L + "qk_w"], a[L + "out_w"], a[L + "fc1_w"],
                         a[L + "fc2_w"].reshape(HIDS, P, CH).transpose(1, 0, 2).reshape(P, HID)], axis=1)
    L = "L0_ffn_"
    shared_down = np.concatenate([a[L + "Ws_down"]] * 2, axis=0)
    m2 = np.concatenate([a[L + "centroids"].T, np.broadcast_to(a[L + "expert_biases"], (P, E0)), a[L + "Ws_up"],
                         shared_down, a[L + "W_up"].transpose(1, 0, 2).reshape(P, E0 * F0),
                         a[L + "W_down"].reshape(PAIRS, P, CH).transpose(1, 0, 2).reshape(P, PAIRS * CH)], axis=1)
    spread = np.zeros((P, P), np.float32)
    spread[0:HEADS] = c["block16"].T
    L = "L1_attn_"
    m3 = np.concatenate([a[L + "Wq"].T, a[L + "Wk"].T, a[L + "Wv"].T, a[L + "Wo"].T, spread,
                         np.broadcast_to(a[L + "bo"], (P, CH))], axis=1)
    return {"x_in": a["L0_attn_x"], "vecs_in": vecs, "m1_in": m1, "m2_in": m2, "pick_in": c["pick"],
            "m3_in": m3, "masks_in": c["masks"],
            "m4_in": np.concatenate([a["L1_ffn_centroids"].T, c["ones"], c["same"], c["before"], c["copies"],
                                     c["offsets"]], axis=1),
            "w1_in": a["L1_ffn_w1"],
            "w2_in": np.ascontiguousarray(a["L1_ffn_w2"].reshape(E1, HIDS1, P, CH).transpose(0, 2, 1, 3)
                                          ).reshape(E1, P, HID1)}


def kernel(**inputs):
    import concourse.bacc as bacc
    from concourse.bass_utils import run_bass_kernel_spmd

    nc = bacc.Bacc("TRN2", target_bir_lowering=False, num_devices=1)
    arrays = {name: np.ascontiguousarray(a) for name, a in layouts(inputs).items()}
    args = [nc.dram_tensor(name, a.shape, mybir.dt.from_np(a.dtype), kind="ExternalInput").ap()
            for name, a in arrays.items()]
    out = nc.dram_tensor("x_out", (BATCH, SEQ, CH), F32, kind="ExternalOutput").ap()
    program(nc, *args, out)
    r = run_bass_kernel_spmd(nc, [arrays], core_ids=[0])
    return r.results[0]["x_out"]
```
